# Optimizing a Trainium2 kernel written in Bass

```python
import numpy as np
import jax
import jax.numpy as jnp

def _softmax(x, axis=-1):
    return jax.nn.softmax(x, axis=axis)

def _gelu(x):
    return jax.nn.gelu(x, approximate=True)

def _silu(x):
    return jax.nn.silu(x)

def _sigmoid(x):
    return jax.nn.sigmoid(x)

def _layernorm(x, axis=-1, eps=1e-05):
    m = jnp.mean(x, axis=axis, keepdims=True)
    v = jnp.var(x, axis=axis, keepdims=True)
    return (x - m) / jnp.sqrt(v + eps)

def _scatter_add(tgt, idx, src, axis=0):
    return tgt.at[idx].add(src)

def _segment_sum(src, seg, n):
    return jax.ops.segment_sum(src, seg, n)
kernel_name = 'mk_lm_tower_d1_tok_ids1024_r4_486aee'

def setup_inputs(seed: int=0):
    np.random.seed(seed)
    _w = jnp.asarray

    def _rec_inputs():
        import jax
        import jax.numpy as jnp
        _rk = jax.random.key(seed)
        x = jax.random.randint(jax.random.fold_in(_rk, 1), (16, 512), 0, 12564, jnp.int32)
        return x
    x = _rec_inputs()

    def _L0_tok_setup():
        import jax, jax.numpy as jnp
        import numpy as np
        HASH_VOCAB = 262144
        BIGRAM_DIM = 128
        MODEL_DIM = 256
        BOS_ID = 1
        key = jax.random.key(seed)
        k_ids, k_emb, k_proj = jax.random.split(key, 3)
        ids = jax.random.randint(k_ids, (4, 2048), 0, 50257, dtype=jnp.int64 if jax.config.jax_enable_x64 else jnp.int32)
        embed = jax.random.normal(k_emb, (HASH_VOCAB, BIGRAM_DIM), dtype=jnp.float32)
        proj_w = jax.random.normal(k_proj, (MODEL_DIM, BIGRAM_DIM), dtype=jnp.float32) * (1.0 / np.sqrt(BIGRAM_DIM))
        return {'ids': ids, 'embed': embed, 'proj_w': proj_w}
    _L0_tok_all = _L0_tok_setup()
    _L0_tok_in = {k: v for k, v in _L0_tok_all.items() if k in ('embed', 'proj_w')}
    del _L0_tok_all

    def _L0_attn_setup():
        import jax, jax.numpy as jnp
        import numpy as np
        B, L, D, H, K = (8, 512, 256, 16, 31)
        D_CONV = D // H
        EPS = 1e-06
        key = jax.random.key(seed)
        ks = jax.random.split(key, 5)
        return {'x': jax.random.normal(ks[0], (B, L, D), dtype=jnp.float32), 'W_pe': jax.random.normal(ks[1], (D_CONV, 2 * K), dtype=jnp.float32) * 0.1, 'b_pe': jnp.zeros((2 * K,), dtype=jnp.float32), 'stt_energy': jnp.ones((1, H, 1, K), dtype=jnp.float32) + 0.02 * jax.random.normal(ks[2], (1, H, 1, K), dtype=jnp.float32), 'W_fc': jax.random.normal(ks[3], (D, D), dtype=jnp.float32) / jnp.sqrt(jnp.float32(D)), 'gamma': jnp.ones((D,), dtype=jnp.float32), 'beta': jnp.zeros((D,), dtype=jnp.float32)}
    _L0_attn_all = _L0_attn_setup()
    _L0_attn_in = {k: v for k, v in _L0_attn_all.items() if k in ('W_pe', 'b_pe', 'stt_energy', 'W_fc', 'gamma', 'beta')}
    del _L0_attn_all

    def _L0_ffn_setup():
        import math
        import jax, jax.numpy as jnp
        import numpy as np
        B, T, D = (4, 1024, 256)
        H = 16
        HD = D // H
        CAP = int(1024 * 0.125)
        DFF = int(D * 4 * 2 / 3)
        EPS = 1e-06

        def rmsnorm(x, g):
            return x * jax.lax.rsqrt(jnp.mean(x * x, axis=-1, keepdims=True) + EPS) * g
        key = jax.random.key(seed)
        ks = jax.random.split(key, 9)
        s = lambda k, shape: jax.random.normal(k, shape, jnp.float32) * 0.02
        return {'x': jax.random.normal(ks[0], (B, T, D), jnp.float32), 'w_router': s(ks[1], (D,)), 'W_qkv': s(ks[2], (3 * D, D)), 'W_out': s(ks[3], (D, D)), 'g1': jnp.ones((D,), jnp.float32), 'g2': jnp.ones((D,), jnp.float32), 'W1': s(ks[4], (DFF, D)), 'W2': s(ks[5], (DFF, D)), 'W3': s(ks[6], (D, DFF))}
    _L0_ffn_all = _L0_ffn_setup()
    _L0_ffn_in = {k: v for k, v in _L0_ffn_all.items() if k in ('w_router', 'W_qkv', 'W_out', 'g1', 'g2', 'W1', 'W2', 'W3')}
    del _L0_ffn_all
    return {'x': x, 'L0_tok_embed': _L0_tok_in['embed'], 'L0_tok_proj_w': _L0_tok_in['proj_w'], 'L0_attn_W_pe': _L0_attn_in['W_pe'], 'L0_attn_b_pe': _L0_attn_in['b_pe'], 'L0_attn_stt_energy': _L0_attn_in['stt_energy'], 'L0_attn_W_fc': _L0_attn_in['W_fc'], 'L0_attn_gamma': _L0_attn_in['gamma'], 'L0_attn_beta': _L0_attn_in['beta'], 'L0_ffn_w_router': _L0_ffn_in['w_router'], 'L0_ffn_W_qkv': _L0_ffn_in['W_qkv'], 'L0_ffn_W_out': _L0_ffn_in['W_out'], 'L0_ffn_g1': _L0_ffn_in['g1'], 'L0_ffn_g2': _L0_ffn_in['g2'], 'L0_ffn_W1': _L0_ffn_in['W1'], 'L0_ffn_W2': _L0_ffn_in['W2'], 'L0_ffn_W3': _L0_ffn_in['W3']}

def reference(x, L0_tok_embed, L0_tok_proj_w, L0_attn_W_pe, L0_attn_b_pe, L0_attn_stt_energy, L0_attn_W_fc, L0_attn_gamma, L0_attn_beta, L0_ffn_w_router, L0_ffn_W_qkv, L0_ffn_W_out, L0_ffn_g1, L0_ffn_g2, L0_ffn_W1, L0_ffn_W2, L0_ffn_W3):
    import jax
    import jax.numpy as jnp

    def _L0_tok_ref(ids, embed, proj_w):
        import jax, jax.numpy as jnp
        import numpy as np
        HASH_VOCAB = 262144
        BIGRAM_DIM = 128
        MODEL_DIM = 256
        BOS_ID = 1
        prev = jnp.concatenate([jnp.full((ids.shape[0], 1), BOS_ID, dtype=ids.dtype), ids[:, :-1]], axis=1)
        hashed = (prev * 263 + ids) % HASH_VOCAB
        emb = embed[hashed]
        return jnp.einsum('bsd,md->bsm', emb, proj_w)

    def _L0_attn_ref(x, W_pe, b_pe, stt_energy, W_fc, gamma, beta):
        import jax, jax.numpy as jnp
        import numpy as np
        B, L, D, H, K = (8, 512, 256, 16, 31)
        D_CONV = D // H
        EPS = 1e-06
        b, l, d_model = x.shape
        d = d_model // H
        residual = x
        avg = jnp.cumsum(x, axis=1) / jnp.arange(1, l + 1, dtype=x.dtype)[None, :, None]
        ci = avg.reshape(b, l, H, d).transpose(0, 2, 1, 3).reshape(b * H, l, d)
        pc = ci @ W_pe + b_pe
        dyn, gate = (pc[..., :K], pc[..., K:])
        stt = jnp.broadcast_to(stt_energy, (b, H, 1, K)).reshape(b * H, 1, K)
        energy = stt + jax.nn.sigmoid(gate) * dyn
        w = jax.nn.softmax(energy, axis=-1)
        t_idx = jnp.arange(l)[:, None]
        k_idx = jnp.arange(K)[None, :]
        w = jnp.where(t_idx + k_idx - (K - 1) >= 0, w, jnp.zeros((), x.dtype))
        padded = jnp.pad(ci, ((0, 0), (K - 1, 0), (0, 0)))
        out = jnp.zeros((b * H, l, d), dtype=x.dtype)
        for kk in range(K):
            out = out + w[:, :, kk:kk + 1] * padded[:, kk:kk + l, :]
        conv_loc = out.reshape(b, H, l, d).transpose(0, 2, 1, 3).reshape(b, l, d_model)
        v = conv_loc @ W_fc.T + residual
        mu = jnp.mean(v, axis=-1, keepdims=True)
        var = jnp.var(v, axis=-1, keepdims=True)
        v = (v - mu) / jnp.sqrt(var + EPS) * gamma + beta
        return v

    def _L0_ffn_ref(x, w_router, W_qkv, W_out, g1, g2, W1, W2, W3):
        import math
        import jax, jax.numpy as jnp
        import numpy as np
        B, T, D = (4, 1024, 256)
        H = 16
        HD = D // H
        CAP = int(1024 * 0.125)
        DFF = int(D * 4 * 2 / 3)
        EPS = 1e-06

        def rmsnorm(x, g):
            return x * jax.lax.rsqrt(jnp.mean(x * x, axis=-1, keepdims=True) + EPS) * g
        Bq, Tq, Dq = x.shape
        scores = x @ w_router
        _, idx = jax.lax.top_k(scores, CAP)
        x_sel = jnp.take_along_axis(x, idx[:, :, None], axis=1)
        h = rmsnorm(x_sel, g1)
        qkv = (h @ W_qkv.T).reshape(Bq, CAP, 3, H, HD)
        q, k, v = jnp.moveaxis(qkv, 2, 0)
        att = jnp.einsum('bqhd,bkhd->bhqk', q, k) / math.sqrt(HD)
        mask = jnp.triu(jnp.ones((CAP, CAP), bool), 1)
        att = jnp.where(mask, -jnp.inf, att)
        att = jax.nn.softmax(att, axis=-1)
        o = jnp.einsum('bhqk,bkhd->bqhd', att, v).reshape(Bq, CAP, Dq)
        x_attn = o @ W_out.T
        h2 = rmsnorm(x_sel + x_attn, g2)
        x_ff = jax.nn.silu(h2 @ W1.T) * (h2 @ W2.T) @ W3.T
        x_proc = x_sel + x_attn + x_ff
        out = x.at[jnp.arange(Bq)[:, None], idx].set(x_proc)
        return out
    h = _L0_tok_ref(x, L0_tok_embed, L0_tok_proj_w)
    h = h + _L0_attn_ref(_layernorm(h, axis=-1), L0_attn_W_pe, L0_attn_b_pe, L0_attn_stt_energy, L0_attn_W_fc, L0_attn_gamma, L0_attn_beta)
    h = h + _L0_ffn_ref(_layernorm(h, axis=-1), L0_ffn_w_router, L0_ffn_W_qkv, L0_ffn_W_out, L0_ffn_g1, L0_ffn_g2, L0_ffn_W1, L0_ffn_W2, L0_ffn_W3)
    return h

_drawn_inputs = setup_inputs


def setup_inputs(seed=0):
    import zlib

    import numpy as np

    out = dict(_drawn_inputs(seed))
    spreads = {'L0_attn_b_pe': (0.0, 0.8),
     'L0_attn_gamma': (1.0, 0.2),
     'L0_attn_beta': (0.0, 0.1),
     'L0_ffn_g1': (1.0, 0.6),
     'L0_ffn_g2': (1.0, 0.6)}
    factors = {'L0_attn_W_pe': 8.0,
     'L0_attn_stt_energy': 8.0,
     'L0_ffn_w_router': 8.0,
     'L0_ffn_W_qkv': 8.0,
     'L0_ffn_W_out': 8.0,
     'L0_ffn_W1': 8.0,
     'L0_ffn_W2': 8.0,
     'L0_ffn_W3': 8.0}
    for name, (base, spread) in spreads.items():
        noise = np.random.default_rng([zlib.crc32(name.encode()), seed]).standard_normal(out[name].shape)
        drawn = base * np.exp(spread * noise) if base else spread * noise
        out[name] = jnp.asarray(drawn.astype(out[name].dtype))
    for name, factor in factors.items():
        out[name] = (out[name] * factor).astype(out[name].dtype)
    return out
```

```python
import concourse.bass as bass
from concourse import mybir
from contextlib import ExitStack


def lm_tower_kernel(
    nc: bass.Bass,
    x: bass.AP,
    embed: bass.AP,
    proj_t: bass.AP,
    w_pe: bass.AP,
    b_pe: bass.AP,
    stt: bass.AP,
    w_fc_t: bass.AP,
    gamma: bass.AP,
    beta: bass.AP,
    w_router: bass.AP,
    w_qkv_t: bass.AP,
    w_out_t: bass.AP,
    g1: bass.AP,
    g2: bass.AP,
    w1_t: bass.AP,
    w2_t: bass.AP,
    w3_t: bass.AP,
    eye_c: bass.AP,
    tri_c: bass.AP,
    inv_c: bass.AP,
    iota_c: bass.AP,
    head_c: bass.AP,
    part_c: bass.AP,
    out: bass.AP,
):
    f32, bf16, i32 = mybir.dt.float32, mybir.dt.bfloat16, mybir.dt.int32
    ALU = mybir.AluOpType
    ACT = mybir.ActivationFunctionType
    AX = mybir.AxisListType.X

    P = 128
    NSEQ, L = x.shape
    NT = L // P
    DE = embed.shape[1]
    D = proj_t.shape[1]
    H = stt.shape[0]
    DC = D // H
    K = stt.shape[1]
    HH = H // 2
    BL = 32
    WIN = 2 * BL
    NB = L // BL
    QB = P // BL
    SKEW = WIN - BL - (K - 1)
    ROW = H * WIN
    NPAIR = H // 2
    CAP = 128
    AH = 16
    FF = w1_t.shape[1]
    FC = -(-FF // P)
    FR = FC // 2
    LAST = FF - (FC - 1) * P
    HASH = embed.shape[0]
    LOW = 512
    assert K + BL - 1 + SKEW <= WIN and D == 2 * P and CAP == P and DE == P

    SEQ_BAND = L * (ROW + 1) + SKEW
    band = nc.dram_tensor("band_scratch", [NSEQ * SEQ_BAND], f32, kind="Internal").ap()
    SEQ_AVG = (L + BL) * D
    avgs = nc.dram_tensor("avg_scratch", [NSEQ * SEQ_AVG], f32, kind="Internal").ap()
    scores = nc.dram_tensor("score_scratch", [NSEQ, NT, P], f32, kind="Internal").ap()

    ctx = ExitStack()
    with ctx:
        def sb(name, shape, dt=f32):
            return ctx.enter_context(nc.sbuf_tensor(name, shape, dt))

        def pb(name, shape, dt=f32):
            return ctx.enter_context(nc.psum_tensor(name, shape, dt))

        def sem(name):
            return ctx.enter_context(nc.semaphore(name))

        eye = sb("eye", [P, P])
        eye_b = sb("eye_b", [P, P], bf16)
        tri = sb("tri", [P, P])
        eq_mask = sb("eq_mask", [P, P])
        inv = sb("inv", [P, L])
        iota = sb("iota", [P, P])
        head_mask = sb("head_mask", [P, 8])
        part = sb("part", [P, 4])
        causal = sb("causal", [P, 4, P], bf16)
        proj = sb("proj", [P, D])
        pe_w = sb("pe_w", [P, 2, HH, K])
        bias_row = sb("bias_row", [3, 2 * K])
        bias_part = sb("bias_part", [3, 3, 2 * K])
        bias_bf = sb("bias_bf", [3, 2, 2 * K], bf16)
        bias3 = sb("bias3", [3, 2, HH, K], bf16)
        ones3 = sb("ones3", [3, P], bf16)
        stt_b = sb("stt_b", [P, H * K])
        fc = sb("fc", [P, 2, D])
        gamma_b = sb("gamma_b", [P, D])
        beta_b = sb("beta_b", [P, D])
        router_b = sb("router_b", [P, D])
        qkv_w = sb("qkv_w", [P, 2, 3 * D])
        wo = sb("wo", [P, 4, D])
        w1 = sb("w1", [P, 2, FC * P])
        w2 = sb("w2", [P, 2, FC * P])
        w3 = sb("w3", [P, FC, D])
        g1_c = sb("g1_c", [P, 2])
        g2_c = sb("g2_c", [P, 2])
        half_neg = sb("half_neg", [P, NT])
        index = sb("index", [P, NSEQ * NT], i32)
        idx_now = sb("idx_now", [P, NT], i32)
        emb = sb("emb", [P, NT, DE])
        emb_t = sb("emb_t", [P, L])
        h = [sb(f"h{p}", [P, NT, D]) for p in range(2)]
        xln = [sb(f"xln{p}", [P, NT, D]) for p in range(2)]
        stat1 = sb("stat1", [P, NT, 6])
        mv1 = sb("mv1", [P, NT, 2])
        var1 = sb("var1", [P, NT])
        rstd1 = sb("rstd1", [P, NT])
        carry = sb("carry", [P, 2, NT])
        avg_t = sb("avg_t", [P, 2, L])
        avg_n = sb("avg_n", [P, 2, NT, P])
        th = sb("th", [P, 2, HH * K])
        en = sb("en", [P, NT, H * K])
        mx = sb("mx", [P, NT, H])
        sums = sb("sums", [P, NT, H])
        recs = sb("recs", [P, NT, H])
        taps = sb("taps", [P, NT, ROW + 1])
        rows = sb("rows", [P, NT, ROW])
        win = sb("win", [P, NB, 2, P])
        win_rows = win[:].rearrange("p b r (c g) -> p b (r c) g", g=NPAIR)
        cols = sb("cols", [P, 2, NPAIR, P])
        conv_t = sb("conv_t", [P, 2, 2, P])
        v = sb("v", [P, NT, D])
        stat2 = sb("stat2", [P, NT, 6])
        mv2 = sb("mv2", [P, NT, 2])
        var2 = sb("var2", [P, NT])
        rstd2 = sb("rstd2", [P, NT])
        stat3 = sb("stat3", [P, NT, 6])
        mv3 = sb("mv3", [P, NT, 2])
        var3 = sb("var3", [P, NT])
        rstd3 = sb("rstd3", [P, NT])
        x2 = [sb(f"x2_{p}", [P, NT, D]) for p in range(2)]
        base = sb("base", [P, NT, D])
        work = base[0:NSEQ * NT].rearrange("p j m -> p (j m)")
        ids, prev, hi9, lo9, hash_i = (work[:, i * P:(i + 1) * P].bitcast(i32) for i in range(5))
        hash_f = work[:, 5 * P:6 * P]
        junk = sb("junk", [P, L])
        sc = [sb(f"sc{p}", [P, NT]) for p in range(2)]
        sc_t = sb("sc_t", [NT, P])
        sc_row = sb("sc_row", [P, L])
        counts = sb("counts", [P, NT, 3])
        rank = sb("rank", [P, NT])
        pick = sb("pick", [P, NT, CAP])
        pick_t = sb("pick_t", [P, NT * P])
        xs = sb("xs", [P, D])
        ss = sb("ss", [P, 2])
        ms = sb("ms", [P, 2])
        rr = sb("rr", [P, 2])
        hn = sb("hn", [P, D])
        h_t = sb("h_t", [P, 2, P])
        q_t = sb("q_t", [P, 2, P])
        k_t = sb("k_t", [P, 2, P])
        k_m = sb("k_m", [P, 2, 8, P])
        v_p = sb("v_p", [P, AH, 32])
        at = sb("at", [P, 2, 4, P])
        amax = sb("amax", [P, AH])
        asum = sb("asum", [P, AH])
        arec = sb("arec", [P, AH])
        at_t = sb("at_t", [P, 4, 4 * P])
        o_t = sb("o_t", [P, 4 * P])
        xat = sb("xat", [P, D])
        y = sb("y", [P, D])
        th2 = sb("th2", [P, FR * P])
        gs = sb("gs", [P, FR * P])
        g_t = sb("g_t", [P, FC, P])
        delta = sb("delta", [P, D])

        xb = pb("xb", [P, 2, 512])
        tb = [pb(f"tb{i}", [P, 512]) for i in range(2)]
        cb = pb("cb", [P, 2, D])
        bb = [pb(f"bb{i}", [P, 512]) for i in range(3)]

        w_load = sem("w_load")
        wset = sem("wset")
        mset = sem("mset")
        pset = sem("pset")
        dset = sem("dset")
        ids_in = sem("ids_in")
        prev_in = sem("prev_in")
        hash_a = sem("hash_a")
        hash_ps = sem("hash_ps")
        scr_zero = sem("scr_zero")
        idx_ready = sem("idx_ready")
        emb_in = sem("emb_in")
        embt_ps = sem("embt_ps")
        embt_sb = sem("embt_sb")
        h_ps = sem("h_ps")
        h_sb = sem("h_sb")
        hstat = sem("hstat")
        hmv = sem("hmv")
        xln_r = sem("xln_r")
        hb_r = sem("hb_r")
        cum_ps = sem("cum_ps")
        carry_r = sem("carry_r")
        avg_r = sem("avg_r")
        avgn_ps = sem("avgn_ps")
        avgn_sb = sem("avgn_sb")
        avgn_out = sem("avgn_out")
        pc_ps = sem("pc_ps")
        tanh_r = sem("tanh_r")
        prod_r = sem("prod_r")
        sttadd_r = sem("sttadd_r")
        mx_r = sem("mx_r")
        sub_r = sem("sub_r")
        exp_r = sem("exp_r")
        sum_r = sem("sum_r")
        rec_r = sem("rec_r")
        taps_r = sem("taps_r")
        band_out = sem("band_out")
        win_in = sem("win_in")
        t_ps = sem("t_ps")
        cols_a = sem("cols_a")
        cols_d = sem("cols_d")
        conv_ps = sem("conv_ps")
        convt_r = sem("convt_r")
        fc_ps = sem("fc_ps")
        v_r = sem("v_r")
        vstat = sem("vstat")
        vmv = sem("vmv")
        u_r = sem("u_r")
        h2_r = sem("h2_r")
        h2stat = sem("h2stat")
        h2mv = sem("h2mv")
        x2_r = sem("x2_r")
        sc_r = sem("sc_r")
        base_r = sem("base_r")
        sct_ps = sem("sct_ps")
        sct_sb = sem("sct_sb")
        sc_out = sem("sc_out")
        scrow_in = sem("scrow_in")
        cnt_r = sem("cnt_r")
        rank_r = sem("rank_r")
        pick_r = sem("pick_r")
        xs_ps = sem("xs_ps")
        pickt_ps = sem("pickt_ps")
        xs_r = sem("xs_r")
        pickt_r = sem("pickt_r")
        hn_r = sem("hn_r")
        hnt_ps = sem("hnt_ps")
        ht_r = sem("ht_r")
        qk_ps = sem("qk_ps")
        v_ps = sem("v_ps")
        q_r = sem("q_r")
        k_r = sem("k_r")
        vp_r = sem("vp_r")
        km_r = sem("km_r")
        att_ps = sem("att_ps")
        amax_r = sem("amax_r")
        asub_r = sem("asub_r")
        aexp_r = sem("aexp_r")
        asum_r = sem("asum_r")
        arec_r = sem("arec_r")
        anorm_r = sem("anorm_r")
        att_tps = sem("att_tps")
        att_tr = sem("att_tr")
        o_ps = sem("o_ps")
        o_r = sem("o_r")
        wo_ps = sem("wo_ps")
        xat_r = sem("xat_r")
        y_r = sem("y_r")
        hn2_r = sem("hn2_r")
        hn2t_ps = sem("hn2t_ps")
        h2t_r = sem("h2t_r")
        up_ps = sem("up_ps")
        th2_r = sem("th2_r")
        gs_r = sem("gs_r")
        gt_r = sem("gt_r")
        dn_ps = sem("dn_ps")
        delta_r = sem("delta_r")
        put_ps = sem("put_ps")
        res_r = sem("res_r")
        out_done = sem("out_done")
        ss_r, ms_r, rr_r = ([sem(f"{n}_r{i}") for i in range(2)] for n in ("ss", "ms", "rr"))
        var_r, rstd_r = ([sem(f"{n}_r{i}") for i in range(3)] for n in ("var", "rstd"))
        row_in = [sem(f"row_in{j}") for j in range(NT)]

        def some(value):
            return not isinstance(value, int) or value > 0

        def settle(eng):
            eng.nop(nofuse=True)

        def bcast(row, n):
            return bass.AP(row.tensor, row.offset, [[0, P], [1, n]])

        block = ctx.enter_context(nc.Block())

        @block.sync
        def _(sp):
            n = [0]

            def load(dst, src, **kw):
                sp.dma_start(dst, src, **kw).then_inc(w_load, 16)
                n[0] += 1

            flat = x.rearrange("a (b c) -> (a b) c", c=P)
            sp.dma_start(ids, flat).then_inc(ids_in, 16)
            sp.dma_start(prev[:, 1:P], flat[:, 0:P - 1]).then_inc(prev_in, 16)
            sp.dma_start(prev[1:NSEQ * NT, 0:1], flat[0:NSEQ * NT - 1, P - 1:P],
                         allow_slow_non_contiguous=True).then_inc(prev_in, 16)
            sp.dma_start(prev[0:1, 0:1], flat[0:1, 0:1]).then_inc(prev_in, 16)
            load(part[:], part_c)
            load(eye[:], eye_c)
            load(tri[:], tri_c)
            load(proj[:], proj_t)
            load(inv[:], bcast(inv_c, L))
            load(iota[:], bcast(iota_c, P))
            load(head_mask[:], head_c)
            load(bias_row[:], bass.AP(b_pe.tensor, 0, [[0, 3], [1, 2 * K]]))
            load(stt_b[:], bcast(stt, H * K))
            load(fc[:], w_fc_t.rearrange("(k p) m -> p k m", p=P))
            load(gamma_b[:], bcast(gamma, D))
            load(beta_b[:], bcast(beta, D))
            load(router_b[:], bcast(w_router, D))
            load(qkv_w[:], w_qkv_t.rearrange("(k p) m -> p k m", p=P))
            load(g1_c[:], g1.rearrange("(k p) -> p k", p=P), allow_slow_non_contiguous=True)
            load(g2_c[:], g2.rearrange("(k p) -> p k", p=P), allow_slow_non_contiguous=True)
            sp.wait_ge(mset, 1)
            for g in range(HH):
                for kind in range(2):
                    load(pe_w[g * DC:(g + 1) * DC, kind, g, :], w_pe[:, kind * K:(kind + 1) * K])
            for a in range(4):
                load(wo[32 * a:32 * a + 16, :, :],
                     w_out_t.rearrange("(g a c) m -> a c g m", g=4, a=4)[a])
            load(w1[:, :, 0:FF], w1_t.rearrange("(k p) m -> p k m", p=P))
            load(w2[:, :, 0:FF], w2_t.rearrange("(k p) m -> p k m", p=P))
            load(w3[:, 0:FC - 1, :], w3_t[0:(FC - 1) * P, :].rearrange("(k p) m -> p k m", p=P))
            load(w3[0:LAST, FC - 1, :], w3_t[(FC - 1) * P:FF, :])
            assert n[0] == N_W_CHECK, n[0]
            for q in range(NSEQ):
                sp.dma_start(bass.AP(avgs.tensor, q * SEQ_AVG, [[D, BL], [1, D]]), taps[0:BL, 0, 0:D])\
                    .then_inc(scr_zero, 16)
            sp.dma_start(bass.AP(band.tensor, 0, [[SEQ_BAND, NSEQ], [1, SKEW]]), taps[0:NSEQ, 0, 0:SKEW])\
                .then_inc(scr_zero, 16)
            sp.wait_ge(scr_zero, 16 * (NSEQ + 1))

            def send_avg(s, p):
                sp.wait_ge(avgn_sb, 4 * s + 4)
                settle(sp)
                for par in range(2):
                    sp.dma_start(seq_ap(avgs, s, SEQ_AVG, BL * D + par * P,
                                                      [[D, P], [P * D, NT], [1, P]]),
                                 avg_n[:, par, :, :]).then_inc(avgn_out, 16)

            def send_band(s, j):
                sp.wait_ge(taps_r, 4 * s + j + 1)
                settle(sp)
                sp.dma_start(seq_ap(band, s, SEQ_BAND, SKEW + j * P * (ROW + 1),
                                    [[ROW + 1, P], [1, ROW + 1]]),
                             taps[:, j, :]).then_inc(band_out, 16)

            def load_mid(s):
                sp.wait_ge(avgn_out, 32 * s + 32)
                settle(sp)
                if some(4 * s):
                    sp.wait_ge(conv_ps, 4 * s)
                settle(sp)
                for par in range(2):
                    sp.dma_start(win[64 * par:64 * par + 64, :, par, :],
                                 seq_ap(avgs, s, SEQ_AVG, par * P, [[D, WIN], [BL * D, NB], [1, P]]))\
                        .then_inc(win_in, 16)
                sp.wait_ge(band_out, 64 * s + 64)
                settle(sp)
                if some(8 * s):
                    sp.wait_ge(t_ps, 8 * s)
                settle(sp)
                for j in range(NT):
                    sp.dma_start(rows[:, j, :],
                                 seq_ap(band, s, SEQ_BAND, j * P * (ROW + 1),
                                        [[BL * (ROW + 1), QB], [ROW, BL], [1, ROW]]))\
                        .then_inc(row_in[j], 16)

            def send_scores(s):
                sp.wait_ge(sct_sb, s + 1)
                settle(sp)
                sp.dma_start(scores[bass.ds(s, 1), :, :].rearrange("a j p -> (a j) p"), sc_t[:])\
                    .then_inc(sc_out, 16)

            def load_scores(s):
                sp.wait_ge(sc_out, 16 * s + 16)
                settle(sp)
                if some(11 * s):
                    sp.wait_ge(cnt_r, 11 * s)
                settle(sp)
                sp.dma_start(sc_row[:], seq_ap(scores, s, L, 0, [[0, P], [1, L]])).then_inc(scrow_in, 16)

            def store(s, r):
                sp.wait_ge(res_r, 2 * s + r + 1)
                settle(sp)
                sp.dma_start(seq_ap(out, s, L * D, 2 * r * P * D, [[D, P], [P * D, 2], [1, D]]),
                             base[:, 2 * r:2 * r + 2, :]).then_inc(out_done, 16)

            def step(s, p, front, mid, back):
                if back:
                    load_scores(s - 2)
                if mid:
                    load_mid(s - 1)
                if front:
                    send_avg(s, p)
                    for j in range(3):
                        send_band(s, j)
                if mid:
                    send_scores(s - 1)
                if front:
                    send_band(s, 3)
                if back:
                    store(s - 2, 0)
                    store(s - 2, 1)

            schedule(sp, step)
            sp.wait_ge(out_done, 32 * NSEQ)

        @block.gpsimd
        def _(gp):
            G = nc.gpsimd

            def gather(s, p):
                gp.wait_ge(idx_ready, s + 1)
                if some(s):
                    gp.wait_ge(embt_ps, s)
                if not isinstance(s, int):
                    settle(gp)
                for j in range(NT):
                    G.indirect_dma_start(emb[:, j, :], None, embed,
                                         bass.IndirectOffsetOnAxis(ap=idx_now[:, j:j + 1], axis=0))\
                        .then_inc(emb_in, 16)

            def norm1(s, p):
                gp.wait_ge(var_r[0], s + 1)
                if some(4 * s):
                    gp.wait_ge(xln_r, 4 * s)
                G.tensor_tensor(rstd1[:], var1[:], half_neg[:], ALU.pow).then_inc(rstd_r[0], 1)
                gp.wait_ge(xln_r, 4 * s + 4)
                G.tensor_tensor(h[p][:], h[p][:], beta_b[:].unsqueeze(1).to_broadcast([P, NT, D]), ALU.add)\
                    .then_inc(hb_r, 1)

            def add_stt(s, j):
                gp.wait_ge(prod_r, 8 * s + 2 * j + 2)
                G.tensor_tensor(en[:, j, :], en[:, j, :], stt_b[:], ALU.add).then_inc(sttadd_r, 1)

            def by_head(a):
                return a.rearrange("p (h k) -> p h k", k=K)

            def sub_max(s, j):
                gp.wait_ge(mx_r, 4 * s + j + 1)
                G.tensor_tensor(by_head(en[:, j, :]), by_head(en[:, j, :]),
                                mx[:, j, :].unsqueeze(2).to_broadcast([P, H, K]), ALU.subtract)\
                    .then_inc(sub_r, 1)

            def normalise(s, j):
                gp.wait_ge(rec_r, 4 * s + j + 1)
                if some(64 * s):
                    gp.wait_ge(band_out, 64 * s)
                G.tensor_tensor(taps[:, j, 0:ROW].rearrange("p (h k) -> p h k", k=WIN)[:, :, 0:K],
                                by_head(en[:, j, :]),
                                recs[:, j, :].unsqueeze(2).to_broadcast([P, H, K]), ALU.mult)\
                    .then_inc(taps_r, 1)

            def norm2(s):
                gp.wait_ge(var_r[1], s + 1)
                if some(4 * s):
                    gp.wait_ge(h2_r, 4 * s)
                G.tensor_tensor(rstd2[:], var2[:], half_neg[:], ALU.pow).then_inc(rstd_r[1], 1)

            def norm3(s):
                gp.wait_ge(var_r[2], s + 1)
                if some(4 * s):
                    gp.wait_ge(x2_r, 4 * s)
                G.tensor_tensor(rstd3[:], var3[:], half_neg[:], ALU.pow).then_inc(rstd_r[2], 1)

            def add_base(s, p):
                gp.wait_ge(x2_r, 4 * s + 4)
                if some(32 * s):
                    gp.wait_ge(out_done, 32 * s)
                G.tensor_tensor(base[:], v[:], x2[p][:], ALU.add).then_inc(base_r, 1)

            def rms(s, i):
                gp.wait_ge(ms_r[i], s + 1)
                if some(s):
                    gp.wait_ge((hn_r, hn2_r)[i], s)
                G.tensor_tensor(rr[:, i:i + 1], ms[:, i:i + 1], half_neg[:, 0:1], ALU.pow)\
                    .then_inc(rr_r[i], 1)

            def mask_keys(s):
                gp.wait_ge(k_r, s + 1)
                if some(4 * s):
                    gp.wait_ge(att_ps, 4 * s)
                for a in range(2):
                    G.tensor_tensor(k_m[:, a, :, :], k_t[:, a, :].unsqueeze(1).to_broadcast([P, 8, P]),
                                    head_mask[:].unsqueeze(2).to_broadcast([P, 8, P]), ALU.mult)\
                        .then_inc(km_r, 1)

            def norm_att(s, g):
                gp.wait_ge(arec_r, 4 * s + g + 1)
                G.tensor_tensor(at[:, g % 2, :, :], at[:, g % 2, :, :],
                                arec[:, 4 * g:4 * g + 4].unsqueeze(2).to_broadcast([P, 4, P]), ALU.mult)\
                    .then_inc(anorm_r, 1)

            def step(s, p, front, mid, back):
                q, r = s - 1, s - 2
                if back:
                    rms(r, 0)
                if front:
                    norm1(s, p)
                if back:
                    mask_keys(r)
                if back:
                    norm_att(r, 0)
                if front:
                    add_stt(s, 0)
                if back:
                    norm_att(r, 1)
                if front:
                    sub_max(s, 0)
                if back:
                    norm_att(r, 2)
                if front:
                    add_stt(s, 1)
                    normalise(s, 0)
                if back:
                    norm_att(r, 3)
                if front:
                    sub_max(s, 1)
                    add_stt(s, 2)
                    normalise(s, 1)
                    sub_max(s, 2)
                    if not isinstance(s, int) or s + 1 < NSEQ:
                        gather(s + 1, 1 - p)
                if mid:
                    norm2(q)
                if back:
                    rms(r, 1)
                if front:
                    add_stt(s, 3)
                    normalise(s, 2)
                    sub_max(s, 3)
                if mid:
                    norm3(q)
                if front:
                    normalise(s, 3)
                if mid:
                    add_base(q, 1 - p)

            G.memset(half_neg[:], -0.5).then_inc(pset, 1)
            G.memset(ones3[:], 1.0).then_inc(pset, 1)
            G.memset(causal[:], 0.0).then_inc(pset, 1)
            gp.wait_ge(pset, 3)
            G.affine_select(out=causal[:], in_=causal[:], compare_op=ALU.is_ge, fill=-1e38, base=0,
                            pattern=[[0, 4], [-1, P]], channel_multiplier=1).then_inc(pset, 1)
            gp.wait_ge(pset, 4)
            gather(0, 0)
            gp.wait_ge(scr_zero, 16 * (NSEQ + 1))
            gp.wait_ge(w_load, 16 * N_W_CHECK)
            schedule(gp, step)

        @block.scalar
        def _(act):
            A = nc.scalar

            def copy(dst, src, name, **kw):
                A.activation(dst, src, ACT.Copy if not kw else ACT.Identity, **kw).then_inc(name, 1)

            def embt(s):
                act.wait_ge(embt_ps, s + 1)
                if some(2 * s):
                    act.wait_ge(h_ps, 2 * s)
                copy(emb_t[:], xb[:, 0, :], embt_sb)

            def h_out(s, p):
                if some(4 * (s - 1)):
                    act.wait_ge(v_r, 4 * (s - 1))
                if some(4 * (s - 1)):
                    act.wait_ge(h2_r, 4 * (s - 1))
                for b in range(2):
                    act.wait_ge(h_ps, 2 * s + b + 1)
                    copy(h[p][:, 2 * b:2 * b + 2, :], xb[:, b, :].rearrange("p (j m) -> p j m", j=2), h_sb)

            def avg_by_token(s):
                if some(32 * s):
                    act.wait_ge(avgn_out, 32 * s)
                for b in range(2):
                    act.wait_ge(avgn_ps, 2 * s + b + 1)
                    for par in range(2):
                        src = xb[:, b, :].rearrange("p (j g r c) -> p j g r c", j=2, r=2, c=DC)[:, :, :, par, :]
                        copy(avg_n[:, par, 2 * b:2 * b + 2, :].rearrange("p j (c g) -> p j g c", c=DC),
                             src, avgn_sb)

            def tanh(s, n):
                act.wait_ge(pc_ps, 8 * s + n + 1)
                if some(8 * s + n - 1):
                    act.wait_ge(prod_r, 8 * s + n - 1)
                A.activation(th[:, n % 2, :], xb[:, n % 2, HH * K:2 * HH * K], ACT.Tanh, scale=0.5)\
                    .then_inc(tanh_r, 1)

            def exp(s, j):
                act.wait_ge(sub_r, 4 * s + j + 1)
                A.activation(en[:, j, :], en[:, j, :], ACT.Exp).then_inc(exp_r, 1)

            def cols_out(s, j):
                act.wait_ge(t_ps, 8 * s + 2 * j + 1)
                if some(4 * s + j - 1):
                    act.wait_ge(conv_ps, 4 * s + j - 1)
                copy(cols[:, j % 2, 0:4, :], tb[0][:].rearrange("p (a b) -> p a b", a=4), cols_a)

            def conv_out(s, j):
                act.wait_ge(conv_ps, 4 * s + j + 1)
                if some(4 * s + j - 1):
                    act.wait_ge(fc_ps, 4 * s + j - 1)
                copy(conv_t[:, j % 2, :, :], cb[:, 0, :].rearrange("p (a b) -> p a b", a=2), convt_r)

            def scores_out(s):
                act.wait_ge(sct_ps, s + 1)
                if some(16 * s):
                    act.wait_ge(sc_out, 16 * s)
                copy(sc_t[:], cb[0:NT, 0, 0:P], sct_sb)

            def picked(s):
                act.wait_ge(xs_ps, s + 1)
                if some(s):
                    act.wait_ge(xat_r, s)
                if some(s):
                    act.wait_ge(y_r, s)
                copy(xs[:], bb[0][:, 0:D], xs_r)
                act.wait_ge(pickt_ps, s + 1)
                if some(2 * s):
                    act.wait_ge(put_ps, 2 * s)
                copy(pick_t[:], bb[1][:], pickt_r)

            def ht(s):
                act.wait_ge(hnt_ps, s + 1)
                for k in range(2):
                    copy(h_t[:, k, :], bb[0][:, k * P:(k + 1) * P], ht_r, scale=g1_c[:, k:k + 1])

            def qkv_out(s):
                act.wait_ge(qk_ps, s + 1)
                if some(2 * s):
                    act.wait_ge(km_r, 2 * s)
                copy(k_t[:], bb[1][:, 256:512].rearrange("p (a b) -> p a b", a=2), k_r)
                copy(q_t[:], bb[1][:, 0:256].rearrange("p (a b) -> p a b", a=2), q_r, scale=(D // AH) ** -0.5)
                act.wait_ge(v_ps, s + 1)
                copy(v_p[:, :, 0:16], bb[2][:, 0:D].rearrange("p (h c) -> p h c", c=16), vp_r)

            def att_exp(s, g):
                act.wait_ge(asub_r, 4 * s + g + 1)
                A.activation(at[:, g % 2, :, :], at[:, g % 2, :, :], ACT.Exp).then_inc(aexp_r, 1)

            def att_t_out(s, g):
                act.wait_ge(att_tps, 4 * s + g + 1)
                if some(s):
                    act.wait_ge(o_ps, s)
                copy(at_t[:, g, :], bb[2][:], att_tr)

            def o_out(s):
                act.wait_ge(o_ps, s + 1)
                copy(o_t[:], bb[0][:], o_r)

            def xat_out(s):
                act.wait_ge(wo_ps, s + 1)
                if some(s):
                    act.wait_ge(delta_r, s)
                copy(xat[:], bb[1][:, 0:D], xat_r)

            def h2t(s):
                act.wait_ge(hn2t_ps, s + 1)
                for k in range(2):
                    copy(h_t[:, k, :], bb[0][:, k * P:(k + 1) * P], h2t_r, scale=g2_c[:, k:k + 1])

            def tanh2(s, r):
                act.wait_ge(up_ps, 2 * s + r + 1)
                if some(2 * s + r):
                    act.wait_ge(gs_r, 2 * s + r)
                A.activation(th2[:], bb[0][:, 0:FR * P], ACT.Tanh, scale=0.5).then_inc(th2_r, 1)

            def step(s, p, front, mid, back):
                q, r = s - 1, s - 2
                if front:
                    embt(s)
                if back:
                    picked(r)
                if front:
                    h_out(s, p)
                if back:
                    ht(r)
                    qkv_out(r)
                if mid:
                    cols_out(q, 0)
                if back:
                    att_exp(r, 0)
                if mid:
                    conv_out(q, 0)
                if front:
                    avg_by_token(s)
                if mid:
                    cols_out(q, 1)
                if back:
                    att_exp(r, 1)
                if front:
                    tanh(s, 0)
                if back:
                    att_t_out(r, 0)
                if mid:
                    conv_out(q, 1)
                if front:
                    tanh(s, 1)
                if mid:
                    cols_out(q, 2)
                if back:
                    att_exp(r, 2)
                    att_t_out(r, 1)
                if front:
                    tanh(s, 2)
                    exp(s, 0)
                if back:
                    att_exp(r, 3)
                    att_t_out(r, 2)
                if mid:
                    conv_out(q, 2)
                if front:
                    tanh(s, 3)
                if mid:
                    cols_out(q, 3)
                if back:
                    att_t_out(r, 3)
                if front:
                    tanh(s, 4)
                    exp(s, 1)
                if mid:
                    conv_out(q, 3)
                if back:
                    o_out(r)
                if front:
                    tanh(s, 5)
                if back:
                    xat_out(r)
                if front:
                    tanh(s, 6)
                    exp(s, 2)
                if back:
                    h2t(r)
                if front:
                    tanh(s, 7)
                if back:
                    tanh2(r, 0)
                    tanh2(r, 1)
                if mid:
                    scores_out(q)
                if front:
                    exp(s, 3)

            act.wait_ge(w_load, 16 * N_W_CHECK)
            schedule(act, step)

        @block.vector
        def _(dve):
            V = nc.vector

            def take_index(s, p):
                if some(64 * s):
                    dve.wait_ge(emb_in, 64 * s)
                V.tensor_copy(idx_now[:], index[:, bass.ds(s * NT, NT)]).then_inc(idx_ready, 1)

            def variance(s, i, stat, mv, stat_t, mv_t, var_t, eps):
                if some(s):
                    dve.wait_ge(rstd_r[i], s)
                dve.wait_ge(stat, 4 * s + 4)
                settle(dve)
                for j in range(NT):
                    V.bn_aggr(mv_t[:, j, :], stat_t[:, j, :]).then_inc(mv, 1)
                dve.wait_ge(mv, 4 * s + 4)
                V.tensor_scalar(var_t[:], mv_t[:, :, 1], eps, None, ALU.add).then_inc(var_r[i], 1)

            def ln1(s, p):
                for j in range(NT):
                    dve.wait_ge(h_sb, 2 * s + j // 2 + 1)
                    V.bn_stats(stat1[:, j, :], h[p][:, j, :]).then_inc(hstat, 1)
                variance(s, 0, hstat, hmv, stat1, mv1, var1, 1e-5)

            def ln1b(s, p):
                dve.wait_ge(rstd_r[0], s + 1)
                for j in range(NT):
                    V.tensor_scalar(xln[p][:, j, :], h[p][:, j, :], mv1[:, j, 0:1], rstd1[:, j:j + 1],
                                    ALU.subtract, ALU.mult).then_inc(xln_r, 1)

            def average(s):
                dve.wait_ge(cum_ps, s + 1)
                V.tensor_copy(carry[:, :, 1:2], xb[:, :, P - 1:P]).then_inc(carry_r, 1)
                V.tensor_tensor(avg_t[:, :, 0:P], xb[:, :, 0:P],
                                inv[:, 0:P].unsqueeze(1).to_broadcast([P, 2, P]), ALU.mult)\
                    .then_inc(avg_r, 1)
                for j in range(1, NT):
                    if some(3 * s + j):
                        dve.wait_ge(carry_r, 3 * s + j)
                    if j + 1 < NT:
                        V.tensor_tensor(carry[:, :, j + 1:j + 2], xb[:, :, (j + 1) * P - 1:(j + 1) * P],
                                        carry[:, :, j:j + 1], ALU.add).then_inc(carry_r, 1)
                    for a in range(2):
                        V.scalar_tensor_tensor(avg_t[:, a, j * P:(j + 1) * P], xb[:, a, j * P:(j + 1) * P],
                                               carry[:, a, j:j + 1], inv[:, j * P:(j + 1) * P],
                                               ALU.add, ALU.mult).then_inc(avg_r, 1)

            def product(s, n):
                dve.wait_ge(tanh_r, 8 * s + n + 1)
                if some(4 * s):
                    dve.wait_ge(taps_r, 4 * s)
                V.scalar_tensor_tensor(en[:, n // 2, (n % 2) * HH * K:(n % 2 + 1) * HH * K], th[:, n % 2, :],
                                       1.0, xb[:, n % 2, 0:HH * K], ALU.add, ALU.mult).then_inc(prod_r, 1)

            def by_head(a):
                return a.rearrange("p (h k) -> p h k", k=K)

            def tap_max(s, j):
                dve.wait_ge(sttadd_r, 4 * s + j + 1)
                V.tensor_reduce(mx[:, j, :], by_head(en[:, j, :]), AX, ALU.max).then_inc(mx_r, 1)

            def tap_sum(s, j):
                dve.wait_ge(exp_r, 4 * s + j + 1)
                V.tensor_reduce(sums[:, j, :], by_head(en[:, j, :]), AX, ALU.add).then_inc(sum_r, 1)
                dve.wait_ge(sum_r, 4 * s + j + 1)
                V.reciprocal(recs[:, j, :], sums[:, j, :]).then_inc(rec_r, 1)

            def cols_out(s, j):
                dve.wait_ge(t_ps, 8 * s + 2 * j + 2)
                if some(4 * s + j - 1):
                    dve.wait_ge(conv_ps, 4 * s + j - 1)
                V.tensor_copy(cols[:, j % 2, 4:8, :], tb[1][:].rearrange("p (a b) -> p a b", a=4))\
                    .then_inc(cols_d, 1)

            def residual(s, p, j):
                dve.wait_ge(fc_ps, 4 * s + j + 1)
                if some(s):
                    dve.wait_ge(base_r, s)
                V.tensor_tensor(v[:, j, :], cb[:, 1, :], xln[p][:, j, :], ALU.add).then_inc(v_r, 1)
                dve.wait_ge(v_r, 4 * s + j + 1)
                V.bn_stats(stat2[:, j, :], v[:, j, :]).then_inc(vstat, 1)

            def ln2(s):
                variance(s, 1, vstat, vmv, stat2, mv2, var2, 1e-6)
                for j in range(NT):
                    dve.wait_ge(vmv, 4 * s + j + 1)
                    V.scalar_tensor_tensor(v[:, j, :], v[:, j, :], mv2[:, j, 0:1], gamma_b[:],
                                           ALU.subtract, ALU.mult).then_inc(u_r, 1)

            def ln2b(s, p):
                dve.wait_ge(rstd_r[1], s + 1)
                dve.wait_ge(hb_r, s + 1)
                for j in range(NT):
                    dve.wait_ge(u_r, 4 * s + j + 1)
                    V.scalar_tensor_tensor(v[:, j, :], v[:, j, :], rstd2[:, j:j + 1], h[p][:, j, :],
                                           ALU.mult, ALU.add).then_inc(h2_r, 1)
                for j in range(NT):
                    dve.wait_ge(h2_r, 4 * s + j + 1)
                    V.bn_stats(stat3[:, j, :], v[:, j, :]).then_inc(h2stat, 1)
                variance(s, 2, h2stat, h2mv, stat3, mv3, var3, 1e-5)

            def ln3(s, p):
                dve.wait_ge(rstd_r[2], s + 1)
                if some(s - 1):
                    dve.wait_ge(base_r, s - 1)
                if some(s - 1):
                    dve.wait_ge(xs_ps, s - 1)
                for j in range(NT):
                    V.tensor_scalar(x2[p][:, j, :], v[:, j, :], mv3[:, j, 0:1], rstd3[:, j:j + 1],
                                    ALU.subtract, ALU.mult).then_inc(x2_r, 1)
                if some(s - 1):
                    dve.wait_ge(sct_ps, s - 1)
                for j in range(NT):
                    dve.wait_ge(x2_r, 4 * s + j + 1)
                    if some(4 * s + j):
                        dve.wait_ge(sc_r, 4 * s + j)
                    V.scalar_tensor_tensor(junk[:, 0:D], x2[p][:, j, :], 1.0, router_b[:], ALU.mult, ALU.mult,
                                           accum_out=sc[p][:, j:j + 1]).then_inc(sc_r, 1)

            def select(s, p):
                dve.wait_ge(scrow_in, 16 * s + 16)
                if some(s):
                    dve.wait_ge(rank_r, s)
                n = 11 * s

                def count(op, lo, hi, j, c):
                    nonlocal n
                    if some(n):
                        dve.wait_ge(cnt_r, n)
                    V.tensor_scalar(junk[:, lo:hi], sc_row[:, lo:hi], sc[p][:, j:j + 1], None, op, ALU.add,
                                    accum_out=counts[:, j, c:c + 1]).then_inc(cnt_r, 1)
                    n = n + 1

                dve.wait_ge(sc_r, 4 * s + 4)
                for j in range(NT):
                    count(ALU.is_gt, j * P, L, j, 0)
                    if j:
                        count(ALU.is_ge, 0, j * P, j, 1)
                    if some(n):
                        dve.wait_ge(cnt_r, n)
                    V.scalar_tensor_tensor(junk[:, 0:P], sc_row[:, j * P:(j + 1) * P], sc[p][:, j:j + 1],
                                           eq_mask[:], ALU.is_equal, ALU.mult,
                                           accum_out=counts[:, j, 2:3]).then_inc(cnt_r, 1)
                    n = n + 1
                if some(n):
                    dve.wait_ge(cnt_r, n)
                if some(4 * s):
                    dve.wait_ge(pick_r, 4 * s)
                V.tensor_reduce(rank[:], counts[:], AX, ALU.add).then_inc(rank_r, 1)
                dve.wait_ge(rank_r, s + 1)
                if some(s):
                    dve.wait_ge(pickt_ps, s)
                for j in range(NT):
                    V.tensor_scalar(pick[:, j, :], iota[:], rank[:, j:j + 1], None, ALU.is_equal)\
                        .then_inc(pick_r, 1)

            def squares(s, src, i):
                if some(s):
                    dve.wait_ge(rr_r[i], s)
                V.scalar_tensor_tensor(junk[:, 0:D], src[:], 1.0, src[:], ALU.mult, ALU.mult,
                                       accum_out=ss[:, i:i + 1]).then_inc(ss_r[i], 1)
                dve.wait_ge(ss_r[i], s + 1)
                V.tensor_scalar(ms[:, i:i + 1], ss[:, i:i + 1], 1.0 / D, 1e-6, ALU.mult, ALU.add)\
                    .then_inc(ms_r[i], 1)
                dve.wait_ge(rr_r[i], s + 1)

            def rms1(s):
                dve.wait_ge(xs_r, s + 1)
                dve.wait_ge(pick_r, 4 * s + 4)
                squares(s, xs, 0)
                if some(s):
                    dve.wait_ge(hnt_ps, s)
                V.tensor_scalar(hn[:], xs[:], rr[:, 0:1], None, ALU.mult).then_inc(hn_r, 1)

            def att_max(s, g):
                dve.wait_ge(att_ps, 4 * s + g + 1)
                bank = bb[g % 2][:].rearrange("p (a b) -> p a b", a=4)
                V.tensor_reduce(amax[:, 4 * g:4 * g + 4], bank, AX, ALU.max).then_inc(amax_r, 1)
                dve.wait_ge(amax_r, 4 * s + g + 1)
                if some(4 * s + g - 1):
                    dve.wait_ge(att_tps, 4 * s + g - 1)
                V.tensor_tensor(at[:, g % 2, :, :], bank, amax[:, 4 * g:4 * g + 4].unsqueeze(2).to_broadcast([P, 4, P]),
                                ALU.subtract).then_inc(asub_r, 1)

            def att_sum(s, g):
                dve.wait_ge(aexp_r, 4 * s + g + 1)
                V.tensor_reduce(asum[:, 4 * g:4 * g + 4], at[:, g % 2, :, :], AX, ALU.add).then_inc(asum_r, 1)
                dve.wait_ge(asum_r, 4 * s + g + 1)
                V.reciprocal(arec[:, 4 * g:4 * g + 4], asum[:, 4 * g:4 * g + 4]).then_inc(arec_r, 1)

            def rms2(s):
                dve.wait_ge(xat_r, s + 1)
                V.tensor_tensor(y[:], xs[:], xat[:], ALU.add).then_inc(y_r, 1)
                dve.wait_ge(y_r, s + 1)
                squares(s, y, 1)
                if some(s):
                    dve.wait_ge(hn2t_ps, s)
                V.tensor_scalar(hn[:], y[:], rr[:, 1:2], None, ALU.mult).then_inc(hn2_r, 1)

            def gate(s, r):
                dve.wait_ge(th2_r, 2 * s + r + 1)
                if some(2 * s + r):
                    dve.wait_ge(gt_r, 2 * s + r)
                V.scalar_tensor_tensor(gs[:], th2[:], 1.0, bb[0][:, 0:FR * P], ALU.add, ALU.mult)\
                    .then_inc(gs_r, 1)
                dve.wait_ge(gs_r, 2 * s + r + 1)
                if some(s):
                    dve.wait_ge(dn_ps, s)
                V.scalar_tensor_tensor(g_t[:, r * FR:(r + 1) * FR, :], gs[:].rearrange("p (a b) -> p a b", a=FR),
                                       0.5, bb[1][:, 0:FR * P].rearrange("p (a b) -> p a b", a=FR),
                                       ALU.mult, ALU.mult).then_inc(gt_r, 1)

            def add_up(s):
                dve.wait_ge(dn_ps, s + 1)
                if some(2 * s):
                    dve.wait_ge(put_ps, 2 * s)
                V.tensor_tensor(delta[:], bb[2][:, 0:D], xat[:], ALU.add).then_inc(delta_r, 1)

            def finish(s):
                dve.wait_ge(base_r, s + 1)
                for b in range(2):
                    dve.wait_ge(put_ps, 2 * s + b + 1)
                    V.tensor_tensor(base[:, 2 * b:2 * b + 2, :], bb[b][:].rearrange("p (j m) -> p j m", j=2),
                                    base[:, 2 * b:2 * b + 2, :], ALU.add).then_inc(res_r, 1)

            def step(s, p, front, mid, back):
                q, r = s - 1, s - 2
                if back:
                    select(r, p)
                if front:
                    if not isinstance(s, int) or s + 1 < NSEQ:
                        take_index(s + 1, 1 - p)
                    ln1(s, p)
                if back:
                    rms1(r)
                if front:
                    ln1b(s, p)
                if mid:
                    cols_out(q, 0)
                if front:
                    average(s)
                if back:
                    att_max(r, 0)
                    att_max(r, 1)
                if mid:
                    residual(q, 1 - p, 0)
                    cols_out(q, 1)
                if front:
                    product(s, 0)
                if back:
                    att_sum(r, 0)
                if mid:
                    residual(q, 1 - p, 1)
                if front:
                    product(s, 1)
                if mid:
                    cols_out(q, 2)
                if back:
                    att_max(r, 2)
                    att_sum(r, 1)
                if front:
                    tap_max(s, 0)
                    product(s, 2)
                if back:
                    att_max(r, 3)
                    att_sum(r, 2)
                if mid:
                    residual(q, 1 - p, 2)
                if front:
                    product(s, 3)
                if mid:
                    cols_out(q, 3)
                if front:
                    tap_sum(s, 0)
                    tap_max(s, 1)
                if back:
                    att_sum(r, 3)
                if front:
                    product(s, 4)
                if mid:
                    residual(q, 1 - p, 3)
                if front:
                    product(s, 5)
                    tap_sum(s, 1)
                    tap_max(s, 2)
                if mid:
                    ln2(q)
                if back:
                    rms2(r)
                if front:
                    product(s, 6)
                if mid:
                    ln2b(q, 1 - p)
                if front:
                    product(s, 7)
                    tap_sum(s, 2)
                    tap_max(s, 3)
                if back:
                    gate(r, 0)
                if mid:
                    ln3(q, 1 - p)
                if back:
                    gate(r, 1)
                if front:
                    tap_sum(s, 3)
                if back:
                    add_up(r)
                    finish(r)

            V.memset(pe_w[:], 0.0)
            V.memset(wo[:], 0.0)
            V.memset(w1[:], 0.0)
            V.memset(w2[:], 0.0)
            V.memset(w3[:], 0.0)
            V.memset(taps[:], 0.0).then_inc(mset, 1)
            V.memset(win[:], 0.0).then_inc(dset, 1)
            V.memset(counts[:], 0.0).then_inc(dset, 1)
            V.memset(v_p[:], 0.0).then_inc(dset, 1)
            dve.wait_ge(w_load, 16 * N_W_CHECK)
            dve.wait_ge(ids_in, 16)
            dve.wait_ge(prev_in, 48)
            c = [0]

            def link(ins):
                ins.then_inc(hash_a, 1)
                c[0] += 1
                dve.wait_ge(hash_a, c[0])

            n64 = NSEQ * NT
            link(V.tensor_scalar(ids, ids, HASH - 1, None, ALU.bitwise_and))
            link(V.tensor_scalar(prev, prev, HASH - 1, None, ALU.bitwise_and))
            link(V.tensor_scalar(part[:, 2:3], part[:, 3:4], -1.0, 1.0, ALU.mult, ALU.add))
            link(V.tensor_scalar(prev[:, 0:1], prev[:, 0:1], part[0:n64, 2:3], part[0:n64, 3:4],
                                 ALU.mult, ALU.add))
            link(V.tensor_scalar(hi9, prev, 9, None, ALU.logical_shift_right))
            link(V.tensor_scalar(lo9, prev, LOW - 1, None, ALU.bitwise_and))
            link(V.tensor_scalar(hi9, hi9, 263.0, None, ALU.mult))
            link(V.tensor_scalar(hi9, hi9, LOW - 1, None, ALU.bitwise_and))
            link(V.tensor_scalar(lo9, lo9, 263.0, None, ALU.mult))
            link(V.scalar_tensor_tensor(hi9, hi9, float(LOW), lo9, ALU.mult, ALU.add))
            link(V.scalar_tensor_tensor(hi9, hi9, 1.0, ids, ALU.mult, ALU.add))
            link(V.tensor_scalar(hi9, hi9, HASH - 1, None, ALU.bitwise_and))
            link(V.tensor_copy(hash_f, hi9))
            dve.wait_ge(hash_ps, 1)
            link(V.tensor_copy(index[:], tb[0][:, 0:n64]))
            take_index(0, 0)
            link(V.tensor_copy(eye_b[:], eye[:]))
            link(V.tensor_tensor(eq_mask[:], tri[:], eye[:], ALU.subtract))
            link(V.tensor_scalar(eq_mask[:], tri[:], -1.0, 1.0, ALU.mult, ALU.add))
            link(V.tensor_scalar(pe_w[:, 0, :, :], pe_w[:, 0, :, :], 0.5, None, ALU.mult))
            link(V.tensor_scalar(bias_row[:, 0:K], bias_row[:, 0:K], 0.5, None, ALU.mult))
            link(V.tensor_copy(bias_bf[:, 0, :], bias_row[:]))
            link(V.tensor_tensor(bias_part[:, 1, :], bias_row[:], bias_bf[:, 0, :], ALU.subtract))
            link(V.tensor_copy(bias_bf[:, 1, :], bias_part[:, 1, :]))
            link(V.tensor_tensor(bias_part[:, 2, :], bias_part[:, 1, :], bias_bf[:, 1, :], ALU.subtract))
            link(V.tensor_scalar(part[:, 2:3], part[:, 0:1], part[:, 1:2], None, ALU.add))
            link(V.tensor_scalar(part[:, 2:3], part[:, 2:3], -1.0, 1.0, ALU.mult, ALU.add))
            link(V.tensor_scalar(bias_part[:, 0, :], bias_bf[:, 0, :], part[0:3, 0:1], None, ALU.mult))
            link(V.scalar_tensor_tensor(bias_part[:, 0, :], bias_bf[:, 1, :], part[0:3, 1:2],
                                        bias_part[:, 0, :], ALU.mult, ALU.add))
            link(V.scalar_tensor_tensor(bias_part[:, 0, :], bias_part[:, 2, :], part[0:3, 2:3],
                                        bias_part[:, 0, :], ALU.mult, ALU.add))
            link(V.tensor_copy(bias3[:], bias_part[:, 0, :].rearrange("p (a k) -> p a k", a=2)
                               .unsqueeze(2).to_broadcast([3, 2, HH, K])))
            V.tensor_copy(junk[0:3, 0:1], bias_row[:, 0:1]).then_inc(wset, 1)
            schedule(dve, step)

        @block.tensor
        def _(pe):
            T = nc.tensor

            def embt(s, p):
                pe.wait_ge(emb_in, 64 * s + 64)
                if some(8 * s):
                    pe.wait_ge(prod_r, 8 * s)
                for j in range(NT):
                    last = T.transpose(xb[:, 0, j * P:(j + 1) * P], emb[:, j, :], eye[:])
                last.then_inc(embt_ps, 1)

            def project(s):
                pe.wait_ge(embt_sb, s + 1)
                for j in range(NT):
                    m = T.matmul(xb[:, j // 2, (j % 2) * D:(j % 2 + 1) * D], emb_t[:, j * P:(j + 1) * P], proj[:],
                                 start=True, stop=True)
                    if j % 2:
                        m.then_inc(h_ps, 1)

            def running(s, p):
                pe.wait_ge(h_sb, 2 * s + 2)
                for j in range(NT):
                    pe.wait_ge(xln_r, 4 * s + j + 1)
                    for a in range(2):
                        m = T.matmul(xb[:, a, j * P:(j + 1) * P], xln[p][:, j, a * P:(a + 1) * P], tri[:],
                                     start=True, stop=True)
                m.then_inc(cum_ps, 1)

            def avg_by_token(s):
                pe.wait_ge(avg_r, 7 * s + 7)
                for b in range(2):
                    for j in range(2 * b, 2 * b + 2):
                        for a in range(2):
                            m = T.transpose(xb[:, b, ((j % 2) * 2 + a) * P:((j % 2) * 2 + a + 1) * P],
                                            avg_t[:, a, j * P:(j + 1) * P], eye[:])
                    m.then_inc(avgn_ps, 1)

            def position(s, n):
                j, a = n // 2, n % 2
                if n < 2:
                    pe.wait_ge(avgn_sb, 4 * s + 2 * n + 2)
                else:
                    if some(8 * s + n - 1):
                        pe.wait_ge(prod_r, 8 * s + n - 1)
                dst = xb[:, n % 2, 0:2 * HH * K]
                T.matmul(dst, avg_t[:, a, j * P:(j + 1) * P], pe_w[:].rearrange("p a h k -> p (a h k)"),
                         start=True, stop=False)
                T.matmul(dst, ones3[:], bias3[:].rearrange("p a h k -> p (a h k)"), start=False, stop=True)\
                    .then_inc(pc_ps, 1)

            def band_t(s, j):
                pe.wait_ge(row_in[j], 16 * s + 16)
                for b in range(2):
                    if some(4 * s + j):
                        pe.wait_ge((cols_a, cols_d)[b], 4 * s + j)
                    for c in range(4):
                        m = T.transpose(tb[b][:, c * P:(c + 1) * P],
                                        rows[:, j, (4 * b + c) * P:(4 * b + c + 1) * P], eye[:])
                    m.then_inc(t_ps, 1)

            def convolve(s, j):
                if j == 0:
                    pe.wait_ge(win_in, 32 * s + 32)
                    if some(s):
                        pe.wait_ge(sct_sb, s)
                if some(4 * s + j):
                    pe.wait_ge(v_r, 4 * s + j)
                pe.wait_ge(cols_a, 4 * s + j + 1)
                pe.wait_ge(cols_d, 4 * s + j + 1)
                for q in range(QB):
                    for a in range(2):
                        for c in range(4):
                            g = 4 * a + c
                            m = T.matmul(cb[32 * c:32 * c + 32, 0, a * P + q * BL:a * P + (q + 1) * BL],
                                         win_rows[:, j * QB + q, :, g],
                                         cols[:, j % 2, g, q * BL:(q + 1) * BL],
                                         start=True, stop=True, tile_position=(0, 32 * c))
                m.then_inc(conv_ps, 1)

            def w_fc(s, j):
                pe.wait_ge(convt_r, 4 * s + j + 1)
                for a in range(2):
                    m = T.matmul(cb[:, 1, :], conv_t[:, j % 2, a, :], fc[:, a, :], start=(a == 0), stop=(a == 1))
                m.then_inc(fc_ps, 1)

            def score_t(s, p):
                pe.wait_ge(sc_r, 4 * s + 4)
                pe.wait_ge(v_r, 4 * s + 4)
                T.transpose(cb[0:NT, 0, 0:P], sc[p][:], eye[:]).then_inc(sct_ps, 1)

            def pick_rows(s, p):
                pe.wait_ge(pick_r, 4 * s + 4)
                if some(2 * s):
                    pe.wait_ge(res_r, 2 * s)
                for j in range(NT):
                    m = T.matmul(bb[0][:, 0:D], pick[:, j, :], x2[p][:, j, :], start=(j == 0), stop=(j == NT - 1))
                m.then_inc(xs_ps, 1)
                for j in range(NT):
                    m = T.transpose(bb[1][:, j * P:(j + 1) * P], pick[:, j, :], eye[:])
                m.then_inc(pickt_ps, 1)

            def turn(s, ready, done):
                pe.wait_ge(ready, s + 1)
                for k in range(2):
                    m = T.transpose(bb[0][:, k * P:(k + 1) * P], hn[:, k * P:(k + 1) * P], eye[:])
                m.then_inc(done, 1)

            def qkv(s):
                pe.wait_ge(ht_r, 2 * s + 2)
                pe.wait_ge(pickt_r, s + 1)
                for c in range(4):
                    for k in range(2):
                        m = T.matmul(bb[1][:, c * P:(c + 1) * P], qkv_w[:, k, c * P:(c + 1) * P], h_t[:, k, :],
                                     start=(k == 0), stop=(k == 1))
                m.then_inc(qk_ps, 1)
                if some(s):
                    pe.wait_ge(delta_r, s)
                for k in range(2):
                    m = T.matmul(bb[2][:, 0:D], h_t[:, k, :], qkv_w[:, k, 2 * D:3 * D], start=(k == 0), stop=(k == 1))
                m.then_inc(v_ps, 1)

            def attend(s, g):
                pe.wait_ge(km_r, 2 * s + g // 2 + 1)
                pe.wait_ge(q_r, s + 1)
                if g == 1:
                    pe.wait_ge(k_r, s + 1)
                if g >= 2:
                    if some(4 * s + g - 1):
                        pe.wait_ge(asub_r, 4 * s + g - 1)
                dst = bb[g % 2][:]
                T.matmul(dst, q_t[:, g // 2, :], k_m[:, g // 2, 4 * (g % 2):4 * (g % 2) + 4, :]
                         .rearrange("p a b -> p (a b)"), start=True, stop=False)
                T.matmul(dst, eye_b[:], causal[:].rearrange("p a b -> p (a b)"), start=False, stop=True)\
                    .then_inc(att_ps, 1)

            def att_t(s, g):
                pe.wait_ge(anorm_r, 4 * s + g + 1)
                if g == 0:
                    pe.wait_ge(vp_r, s + 1)
                else:
                    if some(4 * s + g):
                        pe.wait_ge(att_tr, 4 * s + g)
                for c in range(4):
                    m = T.transpose(bb[2][:, c * P:(c + 1) * P], at[:, g % 2, c, :], eye[:])
                m.then_inc(att_tps, 1)

            def values(s):
                pe.wait_ge(asub_r, 4 * s + 4)
                for g in range(4):
                    pe.wait_ge(att_tr, 4 * s + g + 1)
                    for c in range(4):
                        m = T.matmul(bb[0][32 * c:32 * c + 32, g * P:(g + 1) * P], v_p[:, 4 * g + c, :],
                                     at_t[:, g, c * P:(c + 1) * P], start=True, stop=True,
                                     tile_position=(0, 32 * c))
                m.then_inc(o_ps, 1)

            def w_out(s):
                pe.wait_ge(o_r, s + 1)
                for g in range(4):
                    m = T.matmul(bb[1][:, 0:D], o_t[:, g * P:(g + 1) * P], wo[:, g, :], start=(g == 0), stop=(g == 3))
                m.then_inc(wo_ps, 1)

            def up(s, r):
                pe.wait_ge(h2t_r, 2 * s + 2)
                pe.wait_ge(xat_r, s + 1)
                if some(2 * s + r):
                    pe.wait_ge(gt_r, 2 * s + r)
                for w, b in ((w1, 0), (w2, 1)):
                    for c in range(FR):
                        f = r * FR + c
                        for k in range(2):
                            m = T.matmul(bb[b][:, c * P:(c + 1) * P], w[:, k, f * P:(f + 1) * P], h_t[:, k, :],
                                         start=(k == 0), stop=(k == 1))
                m.then_inc(up_ps, 1)

            def down(s):
                pe.wait_ge(gt_r, 2 * s + 2)
                pe.wait_ge(att_tr, 4 * s + 4)
                for f in range(FC):
                    m = T.matmul(bb[2][:, 0:D], g_t[:, f, :], w3[:, f, :], start=(f == 0), stop=(f == FC - 1))
                m.then_inc(dn_ps, 1)

            def put_back(s):
                pe.wait_ge(delta_r, s + 1)
                pe.wait_ge(pickt_r, s + 1)
                for j in range(NT):
                    m = T.matmul(bb[j // 2][:, (j % 2) * D:(j % 2 + 1) * D], pick_t[:, j * P:(j + 1) * P], delta[:],
                                 start=True, stop=True)
                    if j % 2:
                        m.then_inc(put_ps, 1)

            def step(s, p, front, mid, back):
                q, r = s - 1, s - 2
                if front:
                    embt(s, p)
                if back:
                    pick_rows(r, p)
                if front:
                    project(s)
                if back:
                    turn(r, hn_r, hnt_ps)
                    qkv(r)
                if front:
                    running(s, p)
                if mid:
                    band_t(q, 0)
                if back:
                    attend(r, 0)
                    attend(r, 1)
                if mid:
                    convolve(q, 0)
                if front:
                    avg_by_token(s)
                if mid:
                    w_fc(q, 0)
                    band_t(q, 1)
                if front:
                    position(s, 0)
                if back:
                    att_t(r, 0)
                    attend(r, 2)
                if mid:
                    convolve(q, 1)
                if front:
                    position(s, 1)
                if mid:
                    w_fc(q, 1)
                    band_t(q, 2)
                if back:
                    att_t(r, 1)
                    attend(r, 3)
                if front:
                    position(s, 2)
                if back:
                    att_t(r, 2)
                if mid:
                    convolve(q, 2)
                if front:
                    position(s, 3)
                if mid:
                    w_fc(q, 2)
                    band_t(q, 3)
                if back:
                    att_t(r, 3)
                if front:
                    position(s, 4)
                if mid:
                    convolve(q, 3)
                if back:
                    values(r)
                if front:
                    position(s, 5)
                if mid:
                    w_fc(q, 3)
                if back:
                    w_out(r)
                if front:
                    position(s, 6)
                if back:
                    turn(r, hn2_r, hn2t_ps)
                if front:
                    position(s, 7)
                if back:
                    up(r, 0)
                    up(r, 1)
                if mid:
                    score_t(q, 1 - p)
                if back:
                    down(r)
                    put_back(r)

            pe.wait_ge(w_load, 16 * N_W_CHECK)
            pe.wait_ge(hash_a, 13)
            T.transpose(tb[0][:, 0:NSEQ * NT], hash_f, eye[0:NSEQ * NT, 0:NSEQ * NT]).then_inc(hash_ps, 1)
            pe.wait_ge(wset, 1)
            schedule(pe, step)


N_W_CHECK = 16 + 16 + 4 + 4


def seq_ap(t, s, size, offset, dims):
    flat = t if len(t.shape) == 1 else t.rearrange(
        {2: "a b -> (a b)", 3: "a b c -> (a b c)"}[len(t.shape)])
    part = flat[bass.ds(s * size, size)] if not isinstance(s, int) else flat[s * size:(s + 1) * size]
    return bass.AP(part.tensor, part.offset + offset, dims)


def schedule(eng, step):
    n = 16
    step(0, 0, True, False, False)
    step(1, 1, True, True, False)
    step(2, 0, True, True, True)
    with eng.Fori(1, (n - 2) // 2) as k:
        step(2 * k + 1, 1, True, True, True)
        step(2 * k + 2, 0, True, True, True)
    step(n - 1, 1, True, True, True)
    step(n, 0, False, True, True)
    step(n + 1, 1, False, False, True)


_CONSTS = ["eye", "tri", "inv", "iota", "head", "part"]


def kernel(**inputs):
    import numpy as np
    import concourse.bacc as _bacc
    from concourse.bass_utils import run_bass_kernel_spmd as _run

    nc = _bacc.Bacc("TRN2", target_bir_lowering=False, num_devices=1)
    g = lambda n: np.asarray(inputs[n])
    r = np.arange(128)
    feeds = {
        "x": g("x"),
        "embed": g("L0_tok_embed"),
        "proj_t": g("L0_tok_proj_w").T,
        "w_pe": g("L0_attn_W_pe"),
        "b_pe": g("L0_attn_b_pe"),
        "stt": g("L0_attn_stt_energy").reshape(16, 31),
        "w_fc_t": g("L0_attn_W_fc").T,
        "gamma": g("L0_attn_gamma"),
        "beta": g("L0_attn_beta"),
        "w_router": g("L0_ffn_w_router"),
        "w_qkv_t": g("L0_ffn_W_qkv").T,
        "w_out_t": g("L0_ffn_W_out").T,
        "g1": g("L0_ffn_g1"),
        "g2": g("L0_ffn_g2"),
        "w1_t": g("L0_ffn_W1").T,
        "w2_t": g("L0_ffn_W2").T,
        "w3_t": g("L0_ffn_W3").T,
        "eye_c": np.eye(128, dtype=np.float32),
        "tri_c": np.triu(np.ones((128, 128), np.float32)),
        "inv_c": (1.0 / np.arange(1, 513)).astype(np.float32)[None],
        "iota_c": r.astype(np.float32)[None],
        "head_c": (r[:, None] // 16 == np.arange(8)).astype(np.float32),
        "part_c": np.stack([r == 0, r == 1, r == 2, r % 4 == 0], 1).astype(np.float32),
    }
    arrays, args = {}, []
    for name, a in feeds.items():
        a = np.ascontiguousarray(a)
        arrays[f"in_{name}"] = a
        args.append(nc.dram_tensor(f"in_{name}", a.shape, mybir.dt.from_np(a.dtype), kind="ExternalInput").ap())
    args.append(nc.dram_tensor("out_0", (16, 512, 256), mybir.dt.float32, kind="ExternalOutput").ap())
    lm_tower_kernel(nc, *args)
    res = _run(nc, [arrays], core_ids=[0])
    return res.results[0]["out_0"]
```

```python
import concourse.bass as bass
from concourse import mybir
from contextlib import ExitStack


def lm_tower_kernel(
    nc: bass.Bass,
    x: bass.AP,
    embed: bass.AP,
    proj_t: bass.AP,
    w_pe: bass.AP,
    b_pe: bass.AP,
    stt: bass.AP,
    w_fc_t: bass.AP,
    gamma: bass.AP,
    beta: bass.AP,
    w_router: bass.AP,
    w_qkv_t: bass.AP,
    w_out_t: bass.AP,
    g1: bass.AP,
    g2: bass.AP,
    w1_t: bass.AP,
    w2_t: bass.AP,
    w3_t: bass.AP,
    eye_c: bass.AP,
    tri_c: bass.AP,
    inv_c: bass.AP,
    iota_c: bass.AP,
    head_c: bass.AP,
    part_c: bass.AP,
    out: bass.AP,
):
    f32, bf16, i32 = mybir.dt.float32, mybir.dt.bfloat16, mybir.dt.int32
    ALU = mybir.AluOpType
    ACT = mybir.ActivationFunctionType
    AX = mybir.AxisListType.X

    P = 128
    NSEQ, L = x.shape
    NT = L // P
    DE = embed.shape[1]
    D = proj_t.shape[1]
    H = stt.shape[0]
    DC = D // H
    K = stt.shape[1]
    HH = H // 2
    BL = 32
    WIN = 2 * BL
    NB = L // BL
    QB = P // BL
    SKEW = WIN - BL - (K - 1)
    ROW = H * WIN
    NPAIR = H // 2
    CAP = 128
    AH = 16
    FF = w1_t.shape[1]
    FC = -(-FF // P)
    FR = FC // 2
    LAST = FF - (FC - 1) * P
    HASH = embed.shape[0]
    LOW = 512
    assert K + BL - 1 + SKEW <= WIN and D == 2 * P and CAP == P and DE == P

    SEQ_BAND = L * (ROW + 1) + SKEW
    band = nc.dram_tensor("band_scratch", [NSEQ * SEQ_BAND], f32, kind="Internal").ap()
    SEQ_AVG = (L + BL) * D
    avgs = nc.dram_tensor("avg_scratch", [NSEQ * SEQ_AVG], f32, kind="Internal").ap()
    scores = nc.dram_tensor("score_scratch", [NSEQ, NT, P], f32, kind="Internal").ap()

    ctx = ExitStack()
    with ctx:
        def sb(name, shape, dt=f32):
            return ctx.enter_context(nc.sbuf_tensor(name, shape, dt))

        def pb(name, shape, dt=f32):
            return ctx.enter_context(nc.psum_tensor(name, shape, dt))

        def sem(name):
            return ctx.enter_context(nc.semaphore(name))

        eye = sb("eye", [P, P])
        eye_b = sb("eye_b", [P, P], bf16)
        tri = sb("tri", [P, P])
        eq_mask = sb("eq_mask", [P, P])
        inv = sb("inv", [P, L])
        iota = sb("iota", [P, P])
        head_mask = sb("head_mask", [P, 8])
        part = sb("part", [P, 4])
        causal = sb("causal", [P, 4, P], bf16)
        proj = sb("proj", [P, D])
        pe_w = sb("pe_w", [P, 2, HH, K])
        pe_row = sb("pe_row", [P, 2 * K])
        bias_row = sb("bias_row", [3, 2 * K])
        bias_part = sb("bias_part", [3, 3, 2 * K])
        bias_bf = sb("bias_bf", [3, 2, 2 * K], bf16)
        bias3 = sb("bias3", [3, 2, HH, K], bf16)
        ones3 = sb("ones3", [3, P], bf16)
        stt_b = sb("stt_b", [P, H * K])
        fc = sb("fc", [P, 2, D])
        gamma_b = sb("gamma_b", [P, D])
        beta_b = sb("beta_b", [P, D])
        router_b = sb("router_b", [P, D])
        qkv_w = sb("qkv_w", [P, 2, 3 * D])
        wo = sb("wo", [P, 2, D])
        w1 = sb("w1", [P, 2, FC * P])
        w2 = sb("w2", [P, 2, FC * P])
        w3 = sb("w3", [P, FC, D])
        g1_c = sb("g1_c", [P, 2])
        g2_c = sb("g2_c", [P, 2])
        half_neg = sb("half_neg", [P, NT])
        index = sb("index", [P, NSEQ * NT], i32)
        idx_now = sb("idx_now", [P, NT], i32)
        emb = sb("emb", [P, NT, DE])
        emb_t = sb("emb_t", [P, L])
        h = [sb(f"h{p}", [P, NT, D]) for p in range(2)]
        xln = [sb(f"xln{p}", [P, NT, D]) for p in range(2)]
        stat1 = sb("stat1", [P, NT, 6])
        mv1 = sb("mv1", [P, NT, 2])
        var1 = sb("var1", [P, NT])
        rstd1 = sb("rstd1", [P, NT])
        carry = sb("carry", [P, 2, NT])
        avg_t = sb("avg_t", [P, 2, L])
        avg_n = sb("avg_n", [P, 2, NT, P])
        th = sb("th", [P, 2, HH * K])
        en = sb("en", [P, NT, H * K])
        mx = sb("mx", [P, NT, H])
        sums = sb("sums", [P, NT, H])
        recs = sb("recs", [P, NT, H])
        taps = sb("taps", [P, NT, ROW + 1])
        rows = sb("rows", [P, NT, ROW])
        win = sb("win", [P, NB, 2, P])
        win_rows = win[:].rearrange("p b r (c g) -> p b (r c) g", g=NPAIR)
        cols = sb("cols", [P, 2, NPAIR, P])
        conv_t = sb("conv_t", [P, 2, 2, P])
        v = sb("v", [P, NT, D])
        stat2 = sb("stat2", [P, NT, 6])
        mv2 = sb("mv2", [P, NT, 2])
        var2 = sb("var2", [P, NT])
        rstd2 = sb("rstd2", [P, NT])
        stat3 = sb("stat3", [P, NT, 6])
        mv3 = sb("mv3", [P, NT, 2])
        var3 = sb("var3", [P, NT])
        rstd3 = sb("rstd3", [P, NT])
        x2 = [sb(f"x2_{p}", [P, NT, D]) for p in range(2)]
        base = sb("base", [P, NT, D])
        work = base[0:NSEQ * NT].rearrange("p j m -> p (j m)")
        ids, prev, hi9, lo9 = (work[:, i * P:(i + 1) * P].bitcast(i32) for i in range(4))
        hash_f = work[:, 4 * P:5 * P]
        junk = sb("junk", [P, L])
        junk_eq = sb("junk_eq", [P, P])
        sc = [sb(f"sc{p}", [P, NT]) for p in range(2)]
        sc_t = sb("sc_t", [NT, P])
        sc_row = sb("sc_row", [P, L])
        counts = sb("counts", [P, NT, 3])
        rank = sb("rank", [P, NT])
        pick = sb("pick", [P, NT, CAP])
        pick_t = sb("pick_t", [P, NT * P])
        xs = sb("xs", [P, D])
        ss = sb("ss", [P, 2])
        ms = sb("ms", [P, 2])
        rr = sb("rr", [P, 2])
        hn = sb("hn", [P, D])
        h_t = sb("h_t", [P, 2, P])
        q_t = sb("q_t", [P, 2, P])
        k_t = sb("k_t", [P, 2, P])
        k_m = sb("k_m", [P, 2, 8, P])
        v_p = sb("v_p", [P, AH, 32])
        v_pairs = v_p[:].rearrange("p (g r) c -> p g r c", r=2)
        at = sb("at", [P, 2, 4, P])
        amax = sb("amax", [P, AH])
        asum = sb("asum", [P, AH])
        arec = sb("arec", [P, AH])
        at_t = sb("at_t", [P, 4, 4 * P])
        o_t = sb("o_t", [P, 2, P])
        xat = sb("xat", [P, D])
        y = sb("y", [P, D])
        th2 = sb("th2", [P, FR * P])
        gs = sb("gs", [P, FR * P])
        g_t = sb("g_t", [P, FC, P])
        delta = sb("delta", [P, D])

        xb = pb("xb", [P, 2, 512])
        tb = [pb(f"tb{i}", [P, 512]) for i in range(2)]
        cb = pb("cb", [P, 2, D])
        bb = [pb(f"bb{i}", [P, 512]) for i in range(3)]

        ids_in = sem("ids_in")
        w_front = sem("w_front")
        w_back = sem("w_back")
        mset = sem("mset")
        pset = sem("pset")
        setup_done = sem("setup_done")
        hash_a = sem("hash_a")
        hash_ps = sem("hash_ps")
        scr_zero = sem("scr_zero")
        idx_ready = sem("idx_ready")
        emb_in = sem("emb_in")
        embt_ps = sem("embt_ps")
        embt_sb = sem("embt_sb")
        h_ps = sem("h_ps")
        h_sb = sem("h_sb")
        hstat = sem("hstat")
        hmv = sem("hmv")
        xln_r = sem("xln_r")
        hb_r = sem("hb_r")
        cum_ps = sem("cum_ps")
        carry_r = sem("carry_r")
        avg_r = sem("avg_r")
        avgn_ps = sem("avgn_ps")
        avgn_sb = sem("avgn_sb")
        avgn_out = sem("avgn_out")
        pc_ps = sem("pc_ps")
        tanh_r = sem("tanh_r")
        prod_r = sem("prod_r")
        sttadd_r = sem("sttadd_r")
        mx_r = sem("mx_r")
        sub_r = sem("sub_r")
        exp_r = sem("exp_r")
        sum_r = sem("sum_r")
        rec_r = sem("rec_r")
        taps_r = sem("taps_r")
        win_in = sem("win_in")
        t_ps = sem("t_ps")
        cols_r = sem("cols_r")
        conv_ps = sem("conv_ps")
        convt_r = sem("convt_r")
        fc_ps = sem("fc_ps")
        v_r = sem("v_r")
        vstat = sem("vstat")
        vmv = sem("vmv")
        u_r = sem("u_r")
        h2_r = sem("h2_r")
        h2stat = sem("h2stat")
        h2mv = sem("h2mv")
        x2_r = sem("x2_r")
        sc_r = sem("sc_r")
        base_r = sem("base_r")
        sct_ps = sem("sct_ps")
        sct_sb = sem("sct_sb")
        sc_out = sem("sc_out")
        scrow_in = sem("scrow_in")
        cnt_r = sem("cnt_r")
        rank_r = sem("rank_r")
        pick_r = sem("pick_r")
        xs_ps = sem("xs_ps")
        pickt_ps = sem("pickt_ps")
        xs_r = sem("xs_r")
        pickt_r = sem("pickt_r")
        hn_r = sem("hn_r")
        hnt_ps = sem("hnt_ps")
        ht_r = sem("ht_r")
        qk_ps = sem("qk_ps")
        v_ps = sem("v_ps")
        q_r = sem("q_r")
        k_r = sem("k_r")
        vp_r = sem("vp_r")
        km_r = sem("km_r")
        att_ps = sem("att_ps")
        amax_r = sem("amax_r")
        aexp_r = sem("aexp_r")
        arec_r = sem("arec_r")
        anorm_r = sem("anorm_r")
        att_tps = sem("att_tps")
        att_tr = sem("att_tr")
        o_ps = sem("o_ps")
        o_r = sem("o_r")
        wo_ps = sem("wo_ps")
        xat_r = sem("xat_r")
        y_r = sem("y_r")
        hn2_r = sem("hn2_r")
        hn2t_ps = sem("hn2t_ps")
        h2t_r = sem("h2t_r")
        up1_ps = sem("up1_ps")
        up2_ps = sem("up2_ps")
        th2_r = sem("th2_r")
        gs_r = sem("gs_r")
        gt_r = sem("gt_r")
        dn_ps = sem("dn_ps")
        delta_r = sem("delta_r")
        put_ps = sem("put_ps")
        res_r = sem("res_r")
        out_done = sem("out_done")
        ss_r, ms_r, rr_r = ([sem(f"{n}_r{i}") for i in range(2)] for n in ("ss", "ms", "rr"))
        var_r, rstd_r = ([sem(f"{n}_r{i}") for i in range(3)] for n in ("var", "rstd"))
        band_out = [sem(f"band_out{j}") for j in range(NT)]
        row_in = [sem(f"row_in{j}") for j in range(NT)]

        def some(value):
            return not isinstance(value, int) or value > 0

        def settle(eng):
            eng.nop(nofuse=True)

        def bcast(row, n):
            return bass.AP(row.tensor, row.offset, [[0, P], [1, n]])

        block = ctx.enter_context(nc.Block())

        @block.sync
        def _(sp):
            flat = x.rearrange("a (b c) -> (a b) c", c=P)
            sp.dma_start(ids, flat).then_inc(ids_in, 16)
            sp.dma_start(prev[:, 1:P], flat[:, 0:P - 1]).then_inc(ids_in, 16)
            sp.dma_start(prev[1:NSEQ * NT, 0:1], flat[0:NSEQ * NT - 1, P - 1:P],
                         allow_slow_non_contiguous=True).then_inc(ids_in, 16)
            sp.dma_start(prev[0:1, 0:1], flat[0:1, 0:1]).then_inc(ids_in, 16)
            sp.dma_start(part[:], part_c).then_inc(ids_in, 16)
            sp.dma_start(eye[:], eye_c).then_inc(ids_in, 16)

            def load(done, dst, src, **kw):
                sp.dma_start(dst, src, **kw).then_inc(done, 16)

            load(w_front, proj[:], proj_t)
            load(w_front, tri[:], tri_c)
            load(w_front, inv[:], bcast(inv_c, L))
            load(w_front, pe_row[:], bass.AP(w_pe.tensor, 0, [[0, HH], [2 * K, DC], [1, 2 * K]]))
            load(w_front, head_mask[:], head_c)
            load(w_front, bias_row[:], bass.AP(b_pe.tensor, 0, [[0, 3], [1, 2 * K]]))
            load(w_front, stt_b[:], bcast(stt, H * K))
            load(w_front, beta_b[:], bcast(beta, D))
            load(w_front, fc[:], w_fc_t.rearrange("(k p) m -> p k m", p=P))
            load(w_front, gamma_b[:], bcast(gamma, D))
            load(w_front, router_b[:], bcast(w_router, D))
            load(w_front, iota[:], bcast(iota_c, P))
            sp.wait_ge(mset, 1)
            sp.dma_start(bass.AP(avgs.tensor, 0, [[D, BL], [SEQ_AVG, NSEQ], [1, D]]),
                         taps[0:BL].rearrange("p j m -> p (j m)")[:, 0:NSEQ * D]
                         .rearrange("p (s m) -> p s m", s=NSEQ)).then_inc(scr_zero, 16)
            sp.dma_start(bass.AP(band.tensor, 0, [[SEQ_BAND, NSEQ], [1, SKEW]]), taps[0:NSEQ, 0, 0:SKEW])\
                .then_inc(scr_zero, 16)
            sp.wait_ge(emb_in, 16 * NT)
            load(w_back, qkv_w[:], w_qkv_t.rearrange("(k p) m -> p k m", p=P))
            load(w_back, g1_c[:], g1.rearrange("(k p) -> p k", p=P), allow_slow_non_contiguous=True)
            load(w_back, g2_c[:], g2.rearrange("(k p) -> p k", p=P), allow_slow_non_contiguous=True)
            load(w_back, wo[:], w_out_t.rearrange("(a p) m -> p a m", p=P))
            load(w_back, w1[:, :, 0:FF], w1_t.rearrange("(k p) m -> p k m", p=P))
            load(w_back, w2[:, :, 0:FF], w2_t.rearrange("(k p) m -> p k m", p=P))
            load(w_back, w3[:, 0:FC - 1, :], w3_t[0:(FC - 1) * P, :].rearrange("(k p) m -> p k m", p=P))
            load(w_back, w3[0:LAST, FC - 1, :], w3_t[(FC - 1) * P:FF, :])
            sp.wait_ge(pset, 6)
            sp.wait_ge(scr_zero, 32)

            def send_avg(s):
                sp.wait_ge(avgn_sb, 4 * s + 4)
                settle(sp)
                for par in range(2):
                    sp.dma_start(seq_ap(avgs, s, SEQ_AVG, BL * D + par * P,
                                                      [[D, P], [P * D, NT], [1, P]]),
                                 avg_n[:, par, :, :]).then_inc(avgn_out, 16)

            def send_band(s, j):
                sp.wait_ge(taps_r, 4 * s + j + 1)
                settle(sp)
                sp.dma_start(seq_ap(band, s, SEQ_BAND, SKEW + j * P * (ROW + 1),
                                    [[ROW + 1, P], [1, ROW + 1]]),
                             taps[:, j, :]).then_inc(band_out[j], 16)

            def load_windows(s):
                sp.wait_ge(avgn_out, 32 * s + 32)
                settle(sp)
                if some(4 * s):
                    sp.wait_ge(conv_ps, 4 * s)
                settle(sp)
                for par in range(2):
                    sp.dma_start(win[64 * par:64 * par + 64, :, par, :],
                                 seq_ap(avgs, s, SEQ_AVG, par * P, [[D, WIN], [BL * D, NB], [1, P]]))\
                        .then_inc(win_in, 16)

            def load_rows(s, j):
                sp.wait_ge(band_out[j], 16 * s + 16)
                settle(sp)
                if some(8 * s + 2 * j - 6):
                    sp.wait_ge(t_ps, 8 * s + 2 * j - 6)
                settle(sp)
                sp.dma_start(rows[:, j, :],
                             seq_ap(band, s, SEQ_BAND, j * P * (ROW + 1),
                                    [[BL * (ROW + 1), QB], [ROW, BL], [1, ROW]]))\
                    .then_inc(row_in[j], 16)

            def send_scores(s):
                sp.wait_ge(sct_sb, s + 1)
                settle(sp)
                sp.dma_start(scores[bass.ds(s, 1), :, :].rearrange("a j p -> (a j) p"), sc_t[:])\
                    .then_inc(sc_out, 16)

            def load_scores(s):
                sp.wait_ge(sc_out, 16 * s + 16)
                settle(sp)
                if some(11 * s):
                    sp.wait_ge(cnt_r, 11 * s)
                settle(sp)
                sp.dma_start(sc_row[:], seq_ap(scores, s, L, 0, [[0, P], [1, L]])).then_inc(scrow_in, 16)

            def store(s, r):
                sp.wait_ge(res_r, 2 * s + r + 1)
                settle(sp)
                sp.dma_start(seq_ap(out, s, L * D, 2 * r * P * D, [[D, P], [P * D, 2], [1, D]]),
                             base[:, 2 * r:2 * r + 2, :]).then_inc(out_done, 16)

            def step(t, p, on):
                s0, s1, s2, s3 = t, t - 1, t - 2, t - 3
                p0, p1, p2, p3 = p, 1 - p, p, 1 - p
                if on[1]:
                    send_band(s1, 2)
                    load_rows(s1, 2)
                    send_band(s1, 3)
                    load_rows(s1, 3)
                    send_scores(s1)
                if on[0]:
                    send_avg(s0)
                if on[1]:
                    load_scores(s1)
                if on[0]:
                    send_band(s0, 0)
                    load_windows(s0)
                    load_rows(s0, 0)
                    send_band(s0, 1)
                    load_rows(s0, 1)
                if on[2]:
                    store(s2, 0)
                    store(s2, 1)

            schedule(sp, step)
            sp.wait_ge(out_done, 32 * NSEQ)

        @block.gpsimd
        def _(gp):
            G = nc.gpsimd

            def gather(s):
                gp.wait_ge(idx_ready, s + 1)
                if some(s):
                    gp.wait_ge(embt_ps, s)
                settle(gp)
                for j in range(NT):
                    G.indirect_dma_start(emb[:, j, :], None, embed,
                                         bass.IndirectOffsetOnAxis(ap=idx_now[:, j:j + 1], axis=0))\
                        .then_inc(emb_in, 16)

            def gather_next(s):
                if not isinstance(s, int) or s + 1 < NSEQ:
                    gather(s + 1)

            def rsqrt1(s):
                gp.wait_ge(var_r[0], s + 1)
                if some(4 * s):
                    gp.wait_ge(xln_r, 4 * s)
                G.tensor_tensor(rstd1[:], var1[:], half_neg[:], ALU.pow).then_inc(rstd_r[0], 1)

            def add_beta(s, p, b):
                gp.wait_ge(xln_r, 4 * s + 2 * b + 2)
                G.tensor_tensor(h[p][:, 2 * b:2 * b + 2, :], h[p][:, 2 * b:2 * b + 2, :],
                                beta_b[:].unsqueeze(1).to_broadcast([P, 2, D]), ALU.add).then_inc(hb_r, 1)

            def add_stt(s, j):
                gp.wait_ge(prod_r, 8 * s + 2 * j + 2)
                G.tensor_tensor(en[:, j, :], en[:, j, :], stt_b[:], ALU.add).then_inc(sttadd_r, 1)

            def by_head(a):
                return a.rearrange("p (h k) -> p h k", k=K)

            def sub_max(s, j):
                gp.wait_ge(mx_r, 4 * s + j + 1)
                G.tensor_tensor(by_head(en[:, j, :]), by_head(en[:, j, :]),
                                mx[:, j, :].unsqueeze(2).to_broadcast([P, H, K]), ALU.subtract)\
                    .then_inc(sub_r, 1)

            def normalise(s, j):
                gp.wait_ge(rec_r, 4 * s + j + 1)
                if some(16 * s):
                    gp.wait_ge(band_out[j], 16 * s)
                G.tensor_tensor(taps[:, j, 0:ROW].rearrange("p (h k) -> p h k", k=WIN)[:, :, 0:K],
                                by_head(en[:, j, :]),
                                recs[:, j, :].unsqueeze(2).to_broadcast([P, H, K]), ALU.mult)\
                    .then_inc(taps_r, 1)

            def rsqrt2(s):
                gp.wait_ge(var_r[1], s + 1)
                if some(4 * s):
                    gp.wait_ge(h2_r, 4 * s)
                G.tensor_tensor(rstd2[:], var2[:], half_neg[:], ALU.pow).then_inc(rstd_r[1], 1)

            def rsqrt3(s):
                gp.wait_ge(var_r[2], s + 1)
                if some(4 * s):
                    gp.wait_ge(x2_r, 4 * s)
                G.tensor_tensor(rstd3[:], var3[:], half_neg[:], ALU.pow).then_inc(rstd_r[2], 1)

            def add_base(s, p, b):
                gp.wait_ge(x2_r, 4 * s + 2 * b + 2)
                if some(32 * s):
                    gp.wait_ge(out_done, 32 * s)
                G.tensor_tensor(base[:, 2 * b:2 * b + 2, :], v[:, 2 * b:2 * b + 2, :],
                                x2[p][:, 2 * b:2 * b + 2, :], ALU.add).then_inc(base_r, 1)

            def rms(s, i):
                gp.wait_ge(ms_r[i], s + 1)
                if some(s):
                    gp.wait_ge((hn_r, hn2_r)[i], s)
                G.tensor_tensor(rr[:, i:i + 1], ms[:, i:i + 1], half_neg[:, 0:1], ALU.pow)\
                    .then_inc(rr_r[i], 1)

            def mask_keys(s, g):
                a, m = g // 2, 4 * (g % 2)
                if g == 0:
                    gp.wait_ge(k_r, s + 1)
                if some(4 * s - 3 + g):
                    gp.wait_ge(att_ps, 4 * s - 3 + g)
                G.tensor_tensor(k_m[:, a, m:m + 4, :], k_t[:, a, :].unsqueeze(1).to_broadcast([P, 4, P]),
                                head_mask[:, m:m + 4].unsqueeze(2).to_broadcast([P, 4, P]), ALU.mult)\
                    .then_inc(km_r, 1)

            def norm_att(s, g):
                gp.wait_ge(arec_r, 4 * s + g + 1)
                G.tensor_tensor(at[:, g % 2, :, :], at[:, g % 2, :, :],
                                arec[:, 4 * g:4 * g + 4].unsqueeze(2).to_broadcast([P, 4, P]), ALU.mult)\
                    .then_inc(anorm_r, 1)

            def step(t, p, on):
                s0, s1, s2, s3 = t, t - 1, t - 2, t - 3
                p0, p1, p2, p3 = p, 1 - p, p, 1 - p
                if on[1]:
                    normalise(s1, 3)
                if on[2]:
                    mask_keys(s2, 0)
                    mask_keys(s2, 1)
                if on[0]:
                    rsqrt1(s0)
                if on[2]:
                    mask_keys(s2, 2)
                    mask_keys(s2, 3)
                    norm_att(s2, 0)
                    norm_att(s2, 1)
                if on[1]:
                    rsqrt2(s1)
                if on[0]:
                    add_beta(s0, p0, 0)
                if on[2]:
                    norm_att(s2, 2)
                    norm_att(s2, 3)
                if on[0]:
                    add_beta(s0, p0, 1)
                    add_stt(s0, 0)
                if on[1]:
                    rsqrt3(s1)
                if on[0]:
                    sub_max(s0, 0)
                if on[2]:
                    rms(s2, 1)
                if on[0]:
                    add_stt(s0, 1)
                    normalise(s0, 0)
                    sub_max(s0, 1)
                    add_stt(s0, 2)
                    normalise(s0, 1)
                    sub_max(s0, 2)
                    gather_next(s0)
                    add_stt(s0, 3)
                    normalise(s0, 2)
                    sub_max(s0, 3)
                if on[1]:
                    rms(s1, 0)
                    add_base(s1, p1, 0)
                    add_base(s1, p1, 1)

            G.memset(half_neg[:], -0.5).then_inc(pset, 1)
            G.memset(ones3[:], 1.0).then_inc(pset, 1)
            G.memset(causal[:], 0.0).then_inc(pset, 1)
            gp.wait_ge(pset, 3)
            G.affine_select(out=causal[:], in_=causal[:], compare_op=ALU.is_ge, fill=-1e38, base=0,
                            pattern=[[0, 4], [-1, P]], channel_multiplier=1).then_inc(pset, 1)
            G.memset(win[:], 0.0).then_inc(pset, 1)
            G.memset(v_p[:], 0.0).then_inc(pset, 1)
            gather(0)
            gp.wait_ge(scr_zero, 32)
            gp.wait_ge(w_front, 16 * FRONT_LOADS)
            schedule(gp, step)

        @block.scalar
        def _(act):
            A = nc.scalar

            def copy(dst, src, name, **kw):
                A.activation(dst, src, ACT.Copy if not kw else ACT.Identity, **kw).then_inc(name, 1)

            def embt(s):
                act.wait_ge(embt_ps, s + 1)
                if some(2 * s):
                    act.wait_ge(h_ps, 2 * s)
                copy(emb_t[:], xb[:, 0, :], embt_sb)

            def h_out(s, p):
                if some(4 * (s - 1)):
                    act.wait_ge(v_r, 4 * (s - 1))
                if some(4 * (s - 1)):
                    act.wait_ge(h2_r, 4 * (s - 1))
                for b in range(2):
                    act.wait_ge(h_ps, 2 * s + b + 1)
                    copy(h[p][:, 2 * b:2 * b + 2, :], xb[:, b, :].rearrange("p (j m) -> p j m", j=2), h_sb)

            def avg_by_token(s):
                if some(32 * s):
                    act.wait_ge(avgn_out, 32 * s)
                for b in range(2):
                    act.wait_ge(avgn_ps, 2 * s + b + 1)
                    for par in range(2):
                        src = xb[:, b, :].rearrange("p (j g r c) -> p j g r c", j=2, r=2, c=DC)[:, :, :, par, :]
                        copy(avg_n[:, par, 2 * b:2 * b + 2, :].rearrange("p j (c g) -> p j g c", c=DC),
                             src, avgn_sb)

            def tanh(s, n):
                act.wait_ge(pc_ps, 8 * s + n + 1)
                if some(8 * s + n - 1):
                    act.wait_ge(prod_r, 8 * s + n - 1)
                A.activation(th[:, n % 2, :], xb[:, n % 2, HH * K:2 * HH * K], ACT.Tanh, scale=0.5)\
                    .then_inc(tanh_r, 1)

            def exp(s, j):
                act.wait_ge(sub_r, 4 * s + j + 1)
                A.activation(en[:, j, :], en[:, j, :], ACT.Exp).then_inc(exp_r, 1)

            def cols_out(s, j, b):
                act.wait_ge(t_ps, 8 * s + 2 * j + b + 1)
                if some(4 * s + j - 1):
                    act.wait_ge(conv_ps, 4 * s + j - 1)
                copy(cols[:, j % 2, 4 * b:4 * b + 4, :], tb[b][:].rearrange("p (a b) -> p a b", a=4), cols_r)

            def conv_out(s, j):
                act.wait_ge(conv_ps, 4 * s + j + 1)
                if some(4 * s + j - 1):
                    act.wait_ge(fc_ps, 4 * s + j - 1)
                copy(conv_t[:, j % 2, :, :], cb[:, 0, :].rearrange("p (a b) -> p a b", a=2), convt_r)

            def scores_out(s):
                act.wait_ge(sct_ps, s + 1)
                if some(16 * s):
                    act.wait_ge(sc_out, 16 * s)
                copy(sc_t[:], cb[0:NT, 0, 0:P], sct_sb)

            def xs_out(s):
                act.wait_ge(xs_ps, s + 1)
                if some(s):
                    act.wait_ge(xat_r, s)
                if some(s):
                    act.wait_ge(y_r, s)
                copy(xs[:], bb[0][:, 0:D], xs_r)

            def pickt_out(s):
                act.wait_ge(pickt_ps, s + 1)
                if some(2 * s):
                    act.wait_ge(put_ps, 2 * s)
                copy(pick_t[:], bb[1][:], pickt_r)

            def ht(s):
                act.wait_ge(hnt_ps, s + 1)
                for k in range(2):
                    copy(h_t[:, k, :], bb[0][:, k * P:(k + 1) * P], ht_r, scale=g1_c[:, k:k + 1])

            def qk_out(s):
                act.wait_ge(qk_ps, s + 1)
                if some(4 * s):
                    act.wait_ge(km_r, 4 * s)
                copy(k_t[:], bb[1][:, 256:512].rearrange("p (a b) -> p a b", a=2), k_r)
                copy(q_t[:], bb[1][:, 0:256].rearrange("p (a b) -> p a b", a=2), q_r, scale=(D // AH) ** -0.5)

            def v_out(s):
                act.wait_ge(v_ps, s + 1)
                for r in range(2):
                    copy(v_pairs[:, :, r, 16 * r:16 * r + 16],
                         bb[2][:, 0:D].rearrange("p (g r c) -> p g r c", r=2, c=16)[:, :, r, :], vp_r)

            def att_exp(s, g):
                act.wait_ge(amax_r, 4 * s + g + 1)
                if some(4 * s + g - 1):
                    act.wait_ge(att_tps, 4 * s + g - 1)
                for c in range(4):
                    A.activation(at[:, g % 2, c, :], bb[g % 2][:, c * P:(c + 1) * P], ACT.Exp,
                                 bias=amax[:, 4 * g + c:4 * g + c + 1],
                                 accum_out=asum[:, 4 * g + c:4 * g + c + 1]).then_inc(aexp_r, 1)

            def att_t_out(s, g):
                act.wait_ge(att_tps, 4 * s + g + 1)
                if some(s):
                    act.wait_ge(o_ps, s)
                copy(at_t[:, g, :], bb[2][:], att_tr)

            def o_out(s):
                act.wait_ge(o_ps, s + 1)
                copy(o_t[:], bb[0][:, 0:D].rearrange("p (a b) -> p a b", a=2), o_r)

            def xat_out(s):
                act.wait_ge(wo_ps, s + 1)
                if some(s):
                    act.wait_ge(delta_r, s)
                copy(xat[:], bb[1][:, 0:D], xat_r)

            def h2t(s):
                act.wait_ge(hn2t_ps, s + 1)
                for k in range(2):
                    copy(h_t[:, k, :], bb[0][:, k * P:(k + 1) * P], h2t_r, scale=g2_c[:, k:k + 1])

            def tanh2(s, r):
                act.wait_ge(up1_ps, 2 * s + r + 1)
                if some(2 * s + r):
                    act.wait_ge(gs_r, 2 * s + r)
                A.activation(th2[:], bb[0][:, 0:FR * P], ACT.Tanh, scale=0.5).then_inc(th2_r, 1)

            def step(t, p, on):
                s0, s1, s2, s3 = t, t - 1, t - 2, t - 3
                p0, p1, p2, p3 = p, 1 - p, p, 1 - p
                if isinstance(t, int) and t == 1:
                    act.wait_ge(w_back, 16 * BACK_LOADS)
                if on[1]:
                    tanh(s1, 7)
                    cols_out(s1, 0, 0)
                    cols_out(s1, 0, 1)
                    conv_out(s1, 0)
                if on[2]:
                    xs_out(s2)
                    pickt_out(s2)
                if on[1]:
                    exp(s1, 3)
                if on[0]:
                    embt(s0)
                if on[1]:
                    cols_out(s1, 1, 0)
                    cols_out(s1, 1, 1)
                if on[2]:
                    ht(s2)
                if on[0]:
                    h_out(s0, p0)
                if on[1]:
                    conv_out(s1, 1)
                if on[2]:
                    qk_out(s2)
                    v_out(s2)
                if on[1]:
                    cols_out(s1, 2, 0)
                    cols_out(s1, 2, 1)
                    conv_out(s1, 2)
                if on[2]:
                    att_exp(s2, 0)
                if on[1]:
                    cols_out(s1, 3, 0)
                    cols_out(s1, 3, 1)
                    conv_out(s1, 3)
                if on[2]:
                    att_exp(s2, 1)
                    att_t_out(s2, 0)
                if on[0]:
                    avg_by_token(s0)
                if on[2]:
                    att_exp(s2, 2)
                    att_t_out(s2, 1)
                    att_exp(s2, 3)
                if on[0]:
                    tanh(s0, 0)
                    tanh(s0, 1)
                if on[2]:
                    att_t_out(s2, 2)
                    att_t_out(s2, 3)
                if on[0]:
                    tanh(s0, 2)
                if on[2]:
                    o_out(s2)
                    xat_out(s2)
                if on[0]:
                    exp(s0, 0)
                    tanh(s0, 3)
                if on[1]:
                    scores_out(s1)
                if on[2]:
                    h2t(s2)
                if on[0]:
                    tanh(s0, 4)
                if on[2]:
                    tanh2(s2, 0)
                if on[0]:
                    exp(s0, 1)
                    tanh(s0, 5)
                if on[2]:
                    tanh2(s2, 1)
                if on[0]:
                    tanh(s0, 6)
                    exp(s0, 2)

            act.wait_ge(pset, 6)
            A.activation(th2[:, 0:NT], half_neg[:], ACT.Tanh)
            schedule(act, step)

        @block.vector
        def _(dve):
            V = nc.vector

            def take_index(s):
                if some(64 * s):
                    dve.wait_ge(emb_in, 64 * s)
                V.tensor_copy(idx_now[:], index[:, bass.ds(s * NT, NT)]).then_inc(idx_ready, 1)

            def take_next_index(s):
                if not isinstance(s, int) or s + 1 < NSEQ:
                    take_index(s + 1)

            def variance(s, i, stat, mv, stat_t, mv_t, var_t, eps):
                if some(s):
                    dve.wait_ge(rstd_r[i], s)
                dve.wait_ge(stat, 4 * s + 4)
                settle(dve)
                for j in range(NT):
                    V.bn_aggr(mv_t[:, j, :], stat_t[:, j, :]).then_inc(mv, 1)
                dve.wait_ge(mv, 4 * s + 4)
                V.tensor_scalar(var_t[:], mv_t[:, :, 1], eps, None, ALU.add).then_inc(var_r[i], 1)

            def stats1(s, p, b):
                for j in range(2 * b, 2 * b + 2):
                    dve.wait_ge(h_sb, 2 * s + b + 1)
                    V.bn_stats(stat1[:, j, :], h[p][:, j, :]).then_inc(hstat, 1)

            def var1_of(s):
                variance(s, 0, hstat, hmv, stat1, mv1, var1, 1e-5)

            def norm1(s, p, b):
                dve.wait_ge(rstd_r[0], s + 1)
                if some(4 * (s - 1)):
                    dve.wait_ge(v_r, 4 * (s - 1))
                if some(s - 1):
                    dve.wait_ge(cum_ps, s - 1)
                for j in range(2 * b, 2 * b + 2):
                    V.tensor_scalar(xln[p][:, j, :], h[p][:, j, :], mv1[:, j, 0:1], rstd1[:, j:j + 1],
                                    ALU.subtract, ALU.mult).then_inc(xln_r, 1)

            def average(s):
                dve.wait_ge(cum_ps, s + 1)
                V.tensor_copy(carry[:, :, 1:2], xb[:, :, P - 1:P]).then_inc(carry_r, 1)
                V.tensor_tensor(avg_t[:, :, 0:P], xb[:, :, 0:P],
                                inv[:, 0:P].unsqueeze(1).to_broadcast([P, 2, P]), ALU.mult)\
                    .then_inc(avg_r, 1)
                for j in range(1, NT):
                    if some(3 * s + j):
                        dve.wait_ge(carry_r, 3 * s + j)
                    if j + 1 < NT:
                        V.tensor_tensor(carry[:, :, j + 1:j + 2], xb[:, :, (j + 1) * P - 1:(j + 1) * P],
                                        carry[:, :, j:j + 1], ALU.add).then_inc(carry_r, 1)
                    for a in range(2):
                        V.scalar_tensor_tensor(avg_t[:, a, j * P:(j + 1) * P], xb[:, a, j * P:(j + 1) * P],
                                               carry[:, a, j:j + 1], inv[:, j * P:(j + 1) * P],
                                               ALU.add, ALU.mult).then_inc(avg_r, 1)

            def product(s, n):
                dve.wait_ge(tanh_r, 8 * s + n + 1)
                if some(4 * s):
                    dve.wait_ge(taps_r, 4 * s)
                V.scalar_tensor_tensor(en[:, n // 2, (n % 2) * HH * K:(n % 2 + 1) * HH * K], th[:, n % 2, :],
                                       1.0, xb[:, n % 2, 0:HH * K], ALU.add, ALU.mult).then_inc(prod_r, 1)

            def by_head(a):
                return a.rearrange("p (h k) -> p h k", k=K)

            def tap_max(s, j):
                dve.wait_ge(sttadd_r, 4 * s + j + 1)
                V.tensor_reduce(mx[:, j, :], by_head(en[:, j, :]), AX, ALU.max).then_inc(mx_r, 1)

            def tap_sum(s, j):
                dve.wait_ge(exp_r, 4 * s + j + 1)
                V.tensor_reduce(sums[:, j, :], by_head(en[:, j, :]), AX, ALU.add).then_inc(sum_r, 1)
                dve.wait_ge(sum_r, 4 * s + j + 1)
                V.reciprocal(recs[:, j, :], sums[:, j, :]).then_inc(rec_r, 1)

            def residual(s, p, j):
                dve.wait_ge(fc_ps, 4 * s + j + 1)
                if some(2 * s):
                    dve.wait_ge(base_r, 2 * s)
                if some(4 * s):
                    dve.wait_ge(x2_r, 4 * s)
                V.tensor_tensor(v[:, j, :], cb[:, 1, :], xln[p][:, j, :], ALU.add).then_inc(v_r, 1)
                dve.wait_ge(v_r, 4 * s + j + 1)
                V.bn_stats(stat2[:, j, :], v[:, j, :]).then_inc(vstat, 1)

            def var2_of(s):
                variance(s, 1, vstat, vmv, stat2, mv2, var2, 1e-6)

            def centre(s, b):
                for j in range(2 * b, 2 * b + 2):
                    dve.wait_ge(vmv, 4 * s + j + 1)
                    V.scalar_tensor_tensor(v[:, j, :], v[:, j, :], mv2[:, j, 0:1], gamma_b[:],
                                           ALU.subtract, ALU.mult).then_inc(u_r, 1)

            def join(s, p, b):
                dve.wait_ge(rstd_r[1], s + 1)
                dve.wait_ge(hb_r, 2 * s + b + 1)
                for j in range(2 * b, 2 * b + 2):
                    dve.wait_ge(u_r, 4 * s + j + 1)
                    V.scalar_tensor_tensor(v[:, j, :], v[:, j, :], rstd2[:, j:j + 1], h[p][:, j, :],
                                           ALU.mult, ALU.add).then_inc(h2_r, 1)

            def stats3(s, b):
                for j in range(2 * b, 2 * b + 2):
                    dve.wait_ge(h2_r, 4 * s + j + 1)
                    V.bn_stats(stat3[:, j, :], v[:, j, :]).then_inc(h2stat, 1)

            def var3_of(s):
                variance(s, 2, h2stat, h2mv, stat3, mv3, var3, 1e-5)

            def norm3(s, p, b):
                dve.wait_ge(rstd_r[2], s + 1)
                if some(2 * (s - 1)):
                    dve.wait_ge(base_r, 2 * (s - 1))
                if some(s - 1):
                    dve.wait_ge(xs_ps, s - 1)
                if some(4 * (s - 1)):
                    dve.wait_ge(sc_r, 4 * (s - 1))
                for j in range(2 * b, 2 * b + 2):
                    V.tensor_scalar(x2[p][:, j, :], v[:, j, :], mv3[:, j, 0:1], rstd3[:, j:j + 1],
                                    ALU.subtract, ALU.mult).then_inc(x2_r, 1)

            def score(s, p, b):
                if some(s - 1):
                    dve.wait_ge(sct_ps, s - 1)
                for j in range(2 * b, 2 * b + 2):
                    dve.wait_ge(x2_r, 4 * s + j + 1)
                    if some(4 * s + j - 1):
                        dve.wait_ge(sc_r, 4 * s + j - 1)
                    V.scalar_tensor_tensor(junk[:, (j % 2) * D:(j % 2 + 1) * D], x2[p][:, j, :], 1.0, router_b[:], ALU.mult, ALU.mult,
                                           accum_out=sc[p][:, j:j + 1]).then_inc(sc_r, 1)

            def count_above(s, p, j):
                if j == 0:
                    dve.wait_ge(scrow_in, 16 * s + 16)
                    dve.wait_ge(sc_r, 4 * s + 4)
                    if some(s):
                        dve.wait_ge(rank_r, s)
                n = 11 * s + (0, 2, 5, 8)[j]
                if some(n - 1):
                    dve.wait_ge(cnt_r, n - 1)
                V.tensor_scalar(junk[:, j * P:L], sc_row[:, j * P:L], sc[p][:, j:j + 1], None, ALU.is_gt, ALU.add,
                                accum_out=counts[:, j, 0:1]).then_inc(cnt_r, 1)
                if j:
                    V.tensor_scalar(junk[:, 0:j * P], sc_row[:, 0:j * P], sc[p][:, j:j + 1], None,
                                    ALU.is_ge, ALU.add, accum_out=counts[:, j, 1:2]).then_inc(cnt_r, 1)
                if some(n):
                    dve.wait_ge(cnt_r, n)
                V.scalar_tensor_tensor(junk_eq[:], sc_row[:, j * P:(j + 1) * P], sc[p][:, j:j + 1],
                                       eq_mask[:], ALU.is_equal, ALU.mult,
                                       accum_out=counts[:, j, 2:3]).then_inc(cnt_r, 1)

            def select(s):
                dve.wait_ge(cnt_r, 11 * s + 11)
                if some(4 * s):
                    dve.wait_ge(pick_r, 4 * s)
                V.tensor_reduce(rank[:], counts[:], AX, ALU.add).then_inc(rank_r, 1)
                dve.wait_ge(rank_r, s + 1)
                if some(s):
                    dve.wait_ge(pickt_ps, s)
                for j in range(NT):
                    V.tensor_scalar(pick[:, j, :], iota[:], rank[:, j:j + 1], None, ALU.is_equal)\
                        .then_inc(pick_r, 1)

            def squares(s, src, i):
                if some(s):
                    dve.wait_ge(rr_r[i], s)
                V.scalar_tensor_tensor(junk[:, 0:D], src[:], 1.0, src[:], ALU.mult, ALU.mult,
                                       accum_out=ss[:, i:i + 1]).then_inc(ss_r[i], 1)
                dve.wait_ge(ss_r[i], s + 1)
                V.tensor_scalar(ms[:, i:i + 1], ss[:, i:i + 1], 1.0 / D, 1e-6, ALU.mult, ALU.add)\
                    .then_inc(ms_r[i], 1)

            def rms1(s):
                dve.wait_ge(xs_r, s + 1)
                dve.wait_ge(pick_r, 4 * s + 4)
                squares(s, xs, 0)

            def rms1b(s):
                dve.wait_ge(rr_r[0], s + 1)
                if some(s):
                    dve.wait_ge(hnt_ps, s)
                V.tensor_scalar(hn[:], xs[:], rr[:, 0:1], None, ALU.mult).then_inc(hn_r, 1)

            def att_max(s, g):
                dve.wait_ge(att_ps, 4 * s + g + 1)
                V.tensor_reduce(amax[:, 4 * g:4 * g + 4], bb[g % 2][:].rearrange("p (a b) -> p a b", a=4),
                                AX, ALU.max, negate=True).then_inc(amax_r, 1)

            def att_rec(s, g):
                dve.wait_ge(aexp_r, 16 * s + 4 * g + 4)
                V.reciprocal(arec[:, 4 * g:4 * g + 4], asum[:, 4 * g:4 * g + 4]).then_inc(arec_r, 1)

            def rms2(s):
                dve.wait_ge(xat_r, s + 1)
                V.tensor_tensor(y[:], xs[:], xat[:], ALU.add).then_inc(y_r, 1)
                dve.wait_ge(y_r, s + 1)
                squares(s, y, 1)

            def rms2b(s):
                dve.wait_ge(rr_r[1], s + 1)
                if some(s):
                    dve.wait_ge(hn2t_ps, s)
                V.tensor_scalar(hn[:], y[:], rr[:, 1:2], None, ALU.mult).then_inc(hn2_r, 1)

            def gate(s, r):
                dve.wait_ge(th2_r, 2 * s + r + 1)
                if some(2 * s + r):
                    dve.wait_ge(gt_r, 2 * s + r)
                V.scalar_tensor_tensor(gs[:], th2[:], 1.0, bb[0][:, 0:FR * P], ALU.add, ALU.mult)\
                    .then_inc(gs_r, 1)
                dve.wait_ge(gs_r, 2 * s + r + 1)
                dve.wait_ge(up2_ps, 2 * s + r + 1)
                if some(2 * s):
                    dve.wait_ge(dn_ps, 2 * s)
                V.scalar_tensor_tensor(g_t[:, r * FR:(r + 1) * FR, :], gs[:].rearrange("p (a b) -> p a b", a=FR),
                                       0.5, bb[1][:, 0:FR * P].rearrange("p (a b) -> p a b", a=FR),
                                       ALU.mult, ALU.mult).then_inc(gt_r, 1)

            def add_up(s):
                dve.wait_ge(dn_ps, 2 * s + 2)
                if some(2 * s):
                    dve.wait_ge(put_ps, 2 * s)
                V.tensor_tensor(delta[:], bb[2][:, 0:D], xat[:], ALU.add).then_inc(delta_r, 1)

            def finish(s, b):
                dve.wait_ge(base_r, 2 * s + 2)
                dve.wait_ge(put_ps, 2 * s + b + 1)
                V.tensor_tensor(base[:, 2 * b:2 * b + 2, :], bb[b][:].rearrange("p (j m) -> p j m", j=2),
                                base[:, 2 * b:2 * b + 2, :], ALU.add).then_inc(res_r, 1)

            def step(t, p, on):
                s0, s1, s2, s3 = t, t - 1, t - 2, t - 3
                p0, p1, p2, p3 = p, 1 - p, p, 1 - p
                if on[2]:
                    select(s2)
                if on[1]:
                    product(s1, 6)
                if on[3]:
                    finish(s3, 0)
                    finish(s3, 1)
                if on[1]:
                    product(s1, 7)
                    tap_sum(s1, 2)
                    tap_max(s1, 3)
                if on[2]:
                    rms1(s2)
                    rms1b(s2)
                if on[1]:
                    tap_sum(s1, 3)
                    residual(s1, p1, 0)
                if on[0]:
                    stats1(s0, p0, 0)
                    stats1(s0, p0, 1)
                if on[1]:
                    residual(s1, p1, 1)
                if on[0]:
                    var1_of(s0)
                if on[2]:
                    att_max(s2, 0)
                if on[0]:
                    norm1(s0, p0, 0)
                    norm1(s0, p0, 1)
                if on[2]:
                    att_max(s2, 1)
                if on[0]:
                    take_next_index(s0)
                if on[2]:
                    att_rec(s2, 0)
                if on[1]:
                    residual(s1, p1, 2)
                if on[0]:
                    average(s0)
                if on[2]:
                    att_max(s2, 2)
                    att_rec(s2, 1)
                if on[1]:
                    residual(s1, p1, 3)
                    var2_of(s1)
                    centre(s1, 0)
                    centre(s1, 1)
                if on[2]:
                    att_max(s2, 3)
                    att_rec(s2, 2)
                if on[1]:
                    join(s1, p1, 0)
                if on[2]:
                    att_rec(s2, 3)
                if on[1]:
                    join(s1, p1, 1)
                if on[0]:
                    product(s0, 0)
                    product(s0, 1)
                if on[1]:
                    stats3(s1, 0)
                    stats3(s1, 1)
                    var3_of(s1)
                if on[0]:
                    tap_max(s0, 0)
                    product(s0, 2)
                if on[1]:
                    norm3(s1, p1, 0)
                    norm3(s1, p1, 1)
                    score(s1, p1, 0)
                if on[2]:
                    rms2(s2)
                if on[1]:
                    score(s1, p1, 1)
                if on[2]:
                    rms2b(s2)
                if on[0]:
                    product(s0, 3)
                    tap_sum(s0, 0)
                    tap_max(s0, 1)
                    product(s0, 4)
                if on[2]:
                    gate(s2, 0)
                if on[0]:
                    product(s0, 5)
                    tap_sum(s0, 1)
                if on[1]:
                    count_above(s1, p1, 0)
                if on[0]:
                    tap_max(s0, 2)
                if on[2]:
                    gate(s2, 1)
                if on[1]:
                    count_above(s1, p1, 1)
                    count_above(s1, p1, 2)
                if on[2]:
                    add_up(s2)
                if on[1]:
                    count_above(s1, p1, 3)

            V.memset(taps[:], 0.0)
            V.memset(w1[:, :, FF:FC * P], 0.0)
            V.memset(w2[:, :, FF:FC * P], 0.0)
            V.memset(w3[:, FC - 1, :], 0.0)
            V.memset(counts[:], 0.0).then_inc(mset, 1)
            dve.wait_ge(ids_in, 96)
            c = [0]

            def link(ins):
                ins.then_inc(hash_a, 1)
                c[0] += 1
                dve.wait_ge(hash_a, c[0])

            n64 = NSEQ * NT
            link(V.tensor_scalar(ids, ids, HASH - 1, None, ALU.bitwise_and))
            link(V.tensor_scalar(prev, prev, HASH - 1, None, ALU.bitwise_and))
            link(V.tensor_scalar(part[:, 2:3], part[:, 3:4], -1.0, 1.0, ALU.mult, ALU.add))
            link(V.tensor_scalar(prev[:, 0:1], prev[:, 0:1], part[0:n64, 2:3], part[0:n64, 3:4],
                                 ALU.mult, ALU.add))
            link(V.tensor_scalar(hi9, prev, 9, None, ALU.logical_shift_right))
            link(V.tensor_scalar(lo9, prev, LOW - 1, None, ALU.bitwise_and))
            link(V.tensor_scalar(hi9, hi9, 263.0, None, ALU.mult))
            link(V.tensor_scalar(hi9, hi9, LOW - 1, None, ALU.bitwise_and))
            link(V.tensor_scalar(lo9, lo9, 263.0, None, ALU.mult))
            link(V.scalar_tensor_tensor(hi9, hi9, float(LOW), lo9, ALU.mult, ALU.add))
            link(V.scalar_tensor_tensor(hi9, hi9, 1.0, ids, ALU.mult, ALU.add))
            link(V.tensor_scalar(hi9, hi9, HASH - 1, None, ALU.bitwise_and))
            link(V.tensor_copy(hash_f, hi9))
            dve.wait_ge(hash_ps, 1)
            link(V.tensor_copy(index[:], tb[0][:, 0:n64]))
            take_index(0)
            dve.wait_ge(w_front, 16 * FRONT_LOADS)
            link(V.tensor_copy(eye_b[:], eye[:]))
            link(V.tensor_scalar(eq_mask[:], tri[:], -1.0, 1.0, ALU.mult, ALU.add))
            link(V.tensor_scalar(pe_row[:, 0:K], pe_row[:, 0:K], 0.5, None, ALU.mult))
            for kind in range(2):
                link(V.tensor_tensor(pe_w[:, kind, :, :],
                                     pe_row[:, kind * K:(kind + 1) * K].unsqueeze(1).to_broadcast([P, HH, K]),
                                     head_mask[:].unsqueeze(2).to_broadcast([P, HH, K]), ALU.mult))
            link(V.tensor_scalar(bias_row[:, 0:K], bias_row[:, 0:K], 0.5, None, ALU.mult))
            link(V.tensor_copy(bias_bf[:, 0, :], bias_row[:]))
            link(V.tensor_tensor(bias_part[:, 1, :], bias_row[:], bias_bf[:, 0, :], ALU.subtract))
            link(V.tensor_copy(bias_bf[:, 1, :], bias_part[:, 1, :]))
            link(V.tensor_tensor(bias_part[:, 2, :], bias_part[:, 1, :], bias_bf[:, 1, :], ALU.subtract))
            link(V.tensor_scalar(part[:, 2:3], part[:, 0:1], part[:, 1:2], None, ALU.add))
            link(V.tensor_scalar(part[:, 2:3], part[:, 2:3], -1.0, 1.0, ALU.mult, ALU.add))
            link(V.tensor_scalar(bias_part[:, 0, :], bias_bf[:, 0, :], part[0:3, 0:1], None, ALU.mult))
            link(V.scalar_tensor_tensor(bias_part[:, 0, :], bias_bf[:, 1, :], part[0:3, 1:2],
                                        bias_part[:, 0, :], ALU.mult, ALU.add))
            link(V.scalar_tensor_tensor(bias_part[:, 0, :], bias_part[:, 2, :], part[0:3, 2:3],
                                        bias_part[:, 0, :], ALU.mult, ALU.add))
            link(V.tensor_copy(bias3[:], bias_part[:, 0, :].rearrange("p (a k) -> p a k", a=2)
                               .unsqueeze(2).to_broadcast([3, 2, HH, K])))
            V.tensor_copy(junk[0:3, 0:1], bias_row[:, 0:1]).then_inc(setup_done, 1)
            schedule(dve, step)

        @block.tensor
        def _(pe):
            T = nc.tensor

            def embt(s):
                pe.wait_ge(emb_in, 64 * s + 64)
                if some(8 * s):
                    pe.wait_ge(prod_r, 8 * s)
                for j in range(NT):
                    last = T.transpose(xb[:, 0, j * P:(j + 1) * P], emb[:, j, :], eye[:])
                last.then_inc(embt_ps, 1)

            def project(s):
                pe.wait_ge(embt_sb, s + 1)
                for j in range(NT):
                    m = T.matmul(xb[:, j // 2, (j % 2) * D:(j % 2 + 1) * D], emb_t[:, j * P:(j + 1) * P], proj[:],
                                 start=True, stop=True)
                    if j % 2:
                        m.then_inc(h_ps, 1)

            def running(s, p):
                pe.wait_ge(h_sb, 2 * s + 2)
                for j in range(NT):
                    pe.wait_ge(xln_r, 4 * s + j + 1)
                    for a in range(2):
                        m = T.matmul(xb[:, a, j * P:(j + 1) * P], xln[p][:, j, a * P:(a + 1) * P], tri[:],
                                     start=True, stop=True)
                m.then_inc(cum_ps, 1)

            def avg_by_token(s):
                pe.wait_ge(avg_r, 7 * s + 7)
                for b in range(2):
                    for j in range(2 * b, 2 * b + 2):
                        for a in range(2):
                            m = T.transpose(xb[:, b, ((j % 2) * 2 + a) * P:((j % 2) * 2 + a + 1) * P],
                                            avg_t[:, a, j * P:(j + 1) * P], eye[:])
                    m.then_inc(avgn_ps, 1)

            def position(s, n):
                j, a = n // 2, n % 2
                if n < 2:
                    pe.wait_ge(avgn_sb, 4 * s + 2 * n + 2)
                else:
                    if some(8 * s + n - 1):
                        pe.wait_ge(prod_r, 8 * s + n - 1)
                dst = xb[:, n % 2, 0:2 * HH * K]
                T.matmul(dst, avg_t[:, a, j * P:(j + 1) * P], pe_w[:].rearrange("p a h k -> p (a h k)"),
                         start=True, stop=False)
                T.matmul(dst, ones3[:], bias3[:].rearrange("p a h k -> p (a h k)"), start=False, stop=True)\
                    .then_inc(pc_ps, 1)

            def band_t(s, j):
                pe.wait_ge(row_in[j], 16 * s + 16)
                for b in range(2):
                    if some(8 * s + 2 * j + b - 1):
                        pe.wait_ge(cols_r, 8 * s + 2 * j + b - 1)
                    for c in range(4):
                        m = T.transpose(tb[b][:, c * P:(c + 1) * P],
                                        rows[:, j, (4 * b + c) * P:(4 * b + c + 1) * P], eye[:])
                    m.then_inc(t_ps, 1)

            def convolve(s, j):
                if j == 0:
                    pe.wait_ge(win_in, 32 * s + 32)
                    if some(s):
                        pe.wait_ge(sct_sb, s)
                if some(4 * s + j):
                    pe.wait_ge(v_r, 4 * s + j)
                pe.wait_ge(cols_r, 8 * s + 2 * j + 2)
                for q in range(QB):
                    for a in range(2):
                        for c in range(4):
                            g = 4 * a + c
                            m = T.matmul(cb[32 * c:32 * c + 32, 0, a * P + q * BL:a * P + (q + 1) * BL],
                                         win_rows[:, j * QB + q, :, g],
                                         cols[:, j % 2, g, q * BL:(q + 1) * BL],
                                         start=True, stop=True, tile_position=(0, 32 * c))
                m.then_inc(conv_ps, 1)

            def w_fc(s, j):
                pe.wait_ge(convt_r, 4 * s + j + 1)
                for a in range(2):
                    m = T.matmul(cb[:, 1, :], conv_t[:, j % 2, a, :], fc[:, a, :], start=(a == 0), stop=(a == 1))
                m.then_inc(fc_ps, 1)

            def score_t(s, p):
                pe.wait_ge(sc_r, 4 * s + 4)
                pe.wait_ge(v_r, 4 * s + 4)
                T.transpose(cb[0:NT, 0, 0:P], sc[p][:], eye[:]).then_inc(sct_ps, 1)

            def pick_rows(s, p):
                if some(2 * s):
                    pe.wait_ge(res_r, 2 * s)
                for j in range(NT):
                    pe.wait_ge(pick_r, 4 * s + j + 1)
                    m = T.matmul(bb[0][:, 0:D], pick[:, j, :], x2[p][:, j, :], start=(j == 0), stop=(j == NT - 1))
                m.then_inc(xs_ps, 1)

            def pick_t_rows(s):
                for j in range(NT):
                    m = T.transpose(bb[1][:, j * P:(j + 1) * P], pick[:, j, :], eye[:])
                m.then_inc(pickt_ps, 1)

            def turn(s, ready, done):
                pe.wait_ge(ready, s + 1)
                for k in range(2):
                    m = T.transpose(bb[0][:, k * P:(k + 1) * P], hn[:, k * P:(k + 1) * P], eye[:])
                m.then_inc(done, 1)

            def qk(s):
                pe.wait_ge(ht_r, 2 * s + 2)
                pe.wait_ge(pickt_r, s + 1)
                for c in range(4):
                    for k in range(2):
                        m = T.matmul(bb[1][:, c * P:(c + 1) * P], qkv_w[:, k, c * P:(c + 1) * P], h_t[:, k, :],
                                     start=(k == 0), stop=(k == 1))
                m.then_inc(qk_ps, 1)

            def values_in(s):
                if some(s):
                    pe.wait_ge(delta_r, s)
                for k in range(2):
                    m = T.matmul(bb[2][:, 0:D], h_t[:, k, :], qkv_w[:, k, 2 * D:3 * D], start=(k == 0), stop=(k == 1))
                m.then_inc(v_ps, 1)

            def attend(s, g):
                pe.wait_ge(km_r, 4 * s + g + 1)
                pe.wait_ge(q_r, s + 1)
                if g == 1:
                    pe.wait_ge(k_r, s + 1)
                if g >= 2:
                    if some(16 * s + 4 * g - 4):
                        pe.wait_ge(aexp_r, 16 * s + 4 * g - 4)
                dst = bb[g % 2][:]
                T.matmul(dst, q_t[:, g // 2, :], k_m[:, g // 2, 4 * (g % 2):4 * (g % 2) + 4, :]
                         .rearrange("p a b -> p (a b)"), start=True, stop=False)
                T.matmul(dst, eye_b[:], causal[:].rearrange("p a b -> p (a b)"), start=False, stop=True)\
                    .then_inc(att_ps, 1)

            def att_t(s, g):
                pe.wait_ge(anorm_r, 4 * s + g + 1)
                if g == 0:
                    pe.wait_ge(vp_r, 2 * s + 2)
                else:
                    if some(4 * s + g):
                        pe.wait_ge(att_tr, 4 * s + g)
                for c in range(4):
                    m = T.transpose(bb[2][:, c * P:(c + 1) * P], at[:, g % 2, c, :], eye[:])
                m.then_inc(att_tps, 1)

            def values(s):
                pe.wait_ge(aexp_r, 16 * s + 16)
                for a in range(2):
                    pe.wait_ge(att_tr, 4 * s + 2 * a + 2)
                    for r in range(2):
                        for c in range(4):
                            m = T.matmul(bb[0][32 * c:32 * c + 32, a * P:(a + 1) * P], v_p[:, 8 * a + 2 * c + r, :],
                                         at_t[:, 2 * a + c // 2, (2 * (c % 2) + r) * P:(2 * (c % 2) + r + 1) * P],
                                         start=(r == 0), stop=(r == 1), tile_position=(0, 32 * c))
                m.then_inc(o_ps, 1)

            def w_out(s):
                pe.wait_ge(o_r, s + 1)
                for a in range(2):
                    m = T.matmul(bb[1][:, 0:D], o_t[:, a, :], wo[:, a, :], start=(a == 0), stop=(a == 1))
                m.then_inc(wo_ps, 1)

            def up(s, r, w):
                if r == 0 and w == 0:
                    pe.wait_ge(h2t_r, 2 * s + 2)
                    pe.wait_ge(xat_r, s + 1)
                if w == 0:
                    if some(2 * s + r):
                        pe.wait_ge(gs_r, 2 * s + r)
                else:
                    if some(2 * s + r):
                        pe.wait_ge(gt_r, 2 * s + r)
                for c in range(FR):
                    f = r * FR + c
                    for k in range(2):
                        m = T.matmul(bb[w][:, c * P:(c + 1) * P], (w1, w2)[w][:, k, f * P:(f + 1) * P],
                                     h_t[:, k, :], start=(k == 0), stop=(k == 1))
                m.then_inc((up1_ps, up2_ps)[w], 1)

            def down(s, r):
                pe.wait_ge(gt_r, 2 * s + r + 1)
                if r == 0:
                    pe.wait_ge(att_tr, 4 * s + 4)
                for f in range(r * FR, (r + 1) * FR):
                    m = T.matmul(bb[2][:, 0:D], g_t[:, f, :], w3[:, f, :], start=(f == 0), stop=(f == FC - 1))
                m.then_inc(dn_ps, 1)

            def put_back(s):
                pe.wait_ge(delta_r, s + 1)
                pe.wait_ge(pickt_r, s + 1)
                for j in range(NT):
                    m = T.matmul(bb[j // 2][:, (j % 2) * D:(j % 2 + 1) * D], pick_t[:, j * P:(j + 1) * P], delta[:],
                                 start=True, stop=True)
                    if j % 2:
                        m.then_inc(put_ps, 1)

            def step(t, p, on):
                s0, s1, s2, s3 = t, t - 1, t - 2, t - 3
                p0, p1, p2, p3 = p, 1 - p, p, 1 - p
                if isinstance(t, int) and t == 1:
                    pe.wait_ge(w_back, 16 * BACK_LOADS)
                if on[3]:
                    turn(s3, hn2_r, hn2t_ps)
                if on[1]:
                    position(s1, 5)
                if on[3]:
                    up(s3, 0, 0)
                    up(s3, 0, 1)
                if on[1]:
                    position(s1, 6)
                if on[3]:
                    up(s3, 1, 0)
                    up(s3, 1, 1)
                    down(s3, 0)
                    down(s3, 1)
                if on[1]:
                    position(s1, 7)
                    band_t(s1, 0)
                if on[3]:
                    put_back(s3)
                if on[1]:
                    convolve(s1, 0)
                if on[2]:
                    pick_rows(s2, p2)
                    pick_t_rows(s2)
                if on[0]:
                    embt(s0)
                if on[1]:
                    w_fc(s1, 0)
                    band_t(s1, 1)
                if on[2]:
                    turn(s2, hn_r, hnt_ps)
                if on[0]:
                    project(s0)
                if on[2]:
                    qk(s2)
                if on[1]:
                    convolve(s1, 1)
                if on[2]:
                    values_in(s2)
                if on[1]:
                    w_fc(s1, 1)
                    band_t(s1, 2)
                if on[2]:
                    attend(s2, 0)
                if on[1]:
                    convolve(s1, 2)
                if on[2]:
                    attend(s2, 1)
                if on[1]:
                    w_fc(s1, 2)
                    band_t(s1, 3)
                if on[0]:
                    running(s0, p0)
                if on[2]:
                    att_t(s2, 0)
                if on[1]:
                    convolve(s1, 3)
                if on[2]:
                    attend(s2, 2)
                if on[1]:
                    w_fc(s1, 3)
                if on[0]:
                    avg_by_token(s0)
                if on[2]:
                    att_t(s2, 1)
                    attend(s2, 3)
                if on[0]:
                    position(s0, 0)
                    position(s0, 1)
                if on[2]:
                    att_t(s2, 2)
                    att_t(s2, 3)
                if on[0]:
                    position(s0, 2)
                if on[2]:
                    values(s2)
                    w_out(s2)
                if on[0]:
                    position(s0, 3)
                    position(s0, 4)
                if on[1]:
                    score_t(s1, p1)

            pe.wait_ge(ids_in, 96)
            pe.wait_ge(hash_a, 13)
            T.transpose(tb[0][:, 0:NSEQ * NT], hash_f, eye[0:NSEQ * NT, 0:NSEQ * NT]).then_inc(hash_ps, 1)
            pe.wait_ge(w_front, 16 * FRONT_LOADS)
            pe.wait_ge(setup_done, 1)
            schedule(pe, step)


FRONT_LOADS = 12
BACK_LOADS = 8


def seq_ap(t, s, size, offset, dims):
    flat = t if len(t.shape) == 1 else t.rearrange(
        {2: "a b -> (a b)", 3: "a b c -> (a b c)"}[len(t.shape)])
    part = flat[bass.ds(s * size, size)] if not isinstance(s, int) else flat[s * size:(s + 1) * size]
    return bass.AP(part.tensor, part.offset + offset, dims)


def schedule(eng, step):
    n, stages = 16, 4

    def at(t):
        step(t, t % 2, [0 <= t - k < n for k in range(stages)])

    first = 5
    for t in range(first):
        at(t)
    with eng.Fori(first // 2, (n - 2) // 2) as k:
        step(2 * k + 1, 1, [True] * stages)
        step(2 * k + 2, 0, [True] * stages)
    for t in range(n - 1, n + stages - 1):
        at(t)


_CONSTS = ["eye", "tri", "inv", "iota", "head", "part"]


def kernel(**inputs):
    import numpy as np
    import concourse.bacc as _bacc
    from concourse.bass_utils import run_bass_kernel_spmd as _run

    nc = _bacc.Bacc("TRN2", target_bir_lowering=False, num_devices=1)
    g = lambda n: np.asarray(inputs[n])
    r = np.arange(128)
    feeds = {
        "x": g("x"),
        "embed": g("L0_tok_embed"),
        "proj_t": g("L0_tok_proj_w").T,
        "w_pe": g("L0_attn_W_pe"),
        "b_pe": g("L0_attn_b_pe"),
        "stt": g("L0_attn_stt_energy").reshape(16, 31),
        "w_fc_t": g("L0_attn_W_fc").T,
        "gamma": g("L0_attn_gamma"),
        "beta": g("L0_attn_beta"),
        "w_router": g("L0_ffn_w_router"),
        "w_qkv_t": g("L0_ffn_W_qkv").T,
        "w_out_t": g("L0_ffn_W_out").T,
        "g1": g("L0_ffn_g1"),
        "g2": g("L0_ffn_g2"),
        "w1_t": g("L0_ffn_W1").T,
        "w2_t": g("L0_ffn_W2").T,
        "w3_t": g("L0_ffn_W3").T,
        "eye_c": np.eye(128, dtype=np.float32),
        "tri_c": np.triu(np.ones((128, 128), np.float32)),
        "inv_c": (1.0 / np.arange(1, 513)).astype(np.float32)[None],
        "iota_c": r.astype(np.float32)[None],
        "head_c": (r[:, None] // 16 == np.arange(8)).astype(np.float32),
        "part_c": np.stack([r == 0, r == 1, r == 2, r % 4 == 0], 1).astype(np.float32),
    }
    arrays, args = {}, []
    for name, a in feeds.items():
        a = np.ascontiguousarray(a)
        arrays[f"in_{name}"] = a
        args.append(nc.dram_tensor(f"in_{name}", a.shape, mybir.dt.from_np(a.dtype), kind="ExternalInput").ap())
    args.append(nc.dram_tensor("out_0", (16, 512, 256), mybir.dt.float32, kind="ExternalOutput").ap())
    lm_tower_kernel(nc, *args)
    res = _run(nc, [arrays], core_ids=[0])
    return res.results[0]["out_0"]
```
